# Optimizing a Trainium2 kernel written in Bass

```python
import numpy as np
import jax
import jax.numpy as jnp

def _softmax(x, axis=-1):
    return jax.nn.softmax(x, axis=axis)

def _gelu(x):
    return jax.nn.gelu(x, approximate=True)

def _silu(x):
    return jax.nn.silu(x)

def _sigmoid(x):
    return jax.nn.sigmoid(x)

def _layernorm(x, axis=-1, eps=1e-05):
    m = jnp.mean(x, axis=axis, keepdims=True)
    v = jnp.var(x, axis=axis, keepdims=True)
    return (x - m) / jnp.sqrt(v + eps)

def _scatter_add(tgt, idx, src, axis=0):
    return tgt.at[idx].add(src)

def _segment_sum(src, seg, n):
    return jax.ops.segment_sum(src, seg, n)
kernel_name = 'mk_gnn_resnorm_d2_gnn_r8_08a7a4'

def setup_inputs(seed: int=0):
    np.random.seed(seed)
    _w = jnp.asarray

    def _rec_inputs():
        import jax
        import jax.numpy as jnp
        _gk = jax.random.key(seed)
        x = -0.000202 + 1 * jax.random.normal(jax.random.fold_in(_gk, 1), (6250, 128), jnp.float32)
        _s = jax.random.randint(jax.random.fold_in(_gk, 2), (100000,), 0, 6250, jnp.int32)
        _d = jax.random.randint(jax.random.fold_in(_gk, 3), (100000,), 0, 6250, jnp.int32)
        _loop = jnp.arange(6250, dtype=jnp.int32)
        src = jnp.concatenate([_s, _d, _loop])
        dst = jnp.concatenate([_d, _s, _loop])
        _o = jnp.argsort(dst, stable=True)
        src = src[_o]
        dst = dst[_o]
        edge_type_3 = jax.random.randint(jax.random.fold_in(_gk, 13), (206250,), 0, 3, jnp.int32)
        edge_weight1 = jax.random.uniform(jax.random.fold_in(_gk, 14), (206250, 1), jnp.float32, 0.0, 1)
        return (x, src, dst, edge_type_3, edge_weight1)
    x, src, dst, edge_type_3, edge_weight1 = _rec_inputs()

    def _L0_gnn_setup():
        import jax, jax.numpy as jnp
        import numpy as np
        N_NODES = 6250
        N_EDGES = 37500
        INPUT_DIM = 128
        HIDDEN_DIM = 256
        NUM_HEADS = 8
        HEAD_DIM = HIDDEN_DIM // NUM_HEADS
        NUM_EDGE_TYPES = 3
        key = jax.random.key(seed)
        ks = jax.random.split(key, 12)
        s_in = 1.0 / np.sqrt(INPUT_DIM)
        s_hid = 1.0 / np.sqrt(HIDDEN_DIM)
        return {'node_features': jax.random.normal(ks[0], (N_NODES, INPUT_DIM), jnp.float32), 'edges': jax.random.randint(ks[1], (N_EDGES, 2), 0, N_NODES), 'edge_types': jax.random.randint(ks[2], (N_EDGES,), 0, NUM_EDGE_TYPES), 'Wq': jax.random.normal(ks[3], (HIDDEN_DIM, INPUT_DIM), jnp.float32) * s_in, 'bq': jax.random.normal(ks[4], (HIDDEN_DIM,), jnp.float32) * s_in, 'Wk': jax.random.normal(ks[5], (HIDDEN_DIM, INPUT_DIM), jnp.float32) * s_in, 'bk': jax.random.normal(ks[6], (HIDDEN_DIM,), jnp.float32) * s_in, 'Wv': jax.random.normal(ks[7], (HIDDEN_DIM, INPUT_DIM), jnp.float32) * s_in, 'bv': jax.random.normal(ks[8], (HIDDEN_DIM,), jnp.float32) * s_in, 'edge_emb': jax.random.normal(ks[9], (NUM_EDGE_TYPES, HIDDEN_DIM), jnp.float32), 'Wo': jax.random.normal(ks[10], (INPUT_DIM, HIDDEN_DIM), jnp.float32) * s_hid, 'bo': jax.random.normal(ks[11], (INPUT_DIM,), jnp.float32) * s_hid}
    _L0_gnn_all = _L0_gnn_setup()
    _L0_gnn_in = {k: v for k, v in _L0_gnn_all.items() if k in ('Wq', 'bq', 'Wk', 'bk', 'Wv', 'bv', 'edge_emb', 'Wo', 'bo')}
    del _L0_gnn_all

    def _L1_gnn_setup():
        import jax, jax.numpy as jnp
        import numpy as np
        N_NODES = 12500
        N_EDGES = 200000
        DIM = 128

        def _gcn_layer(x, row, col, ew, W, b):
            n = x.shape[0]
            h = x @ W.T + b
            ones = jnp.ones_like(ew)
            deg = jax.ops.segment_sum(ones, col, num_segments=n)
            dinv = jnp.where(deg > 0, deg ** (-0.5), 0.0)
            norm = dinv[row] * ew * dinv[col]
            msgs = norm[:, None] * h[row]
            return jax.ops.segment_sum(msgs, col, num_segments=n)
        key = jax.random.key(seed)
        ks = jax.random.split(key, 8)
        x = jax.random.normal(ks[0], (N_NODES, DIM), dtype=jnp.float32)
        row = jax.random.randint(ks[1], (N_EDGES,), 0, N_NODES)
        off = jax.random.randint(ks[2], (N_EDGES,), 1, N_NODES)
        col = (row + off) % N_NODES
        edge_index = jnp.stack([row, col]).astype(jnp.int64)
        edge_weight = jax.random.uniform(ks[3], (N_EDGES, 1), dtype=jnp.float32)
        s = 1.0 / np.sqrt(DIM)
        W1 = jax.random.uniform(ks[4], (DIM, DIM), jnp.float32, -s, s)
        b1 = jax.random.uniform(ks[5], (DIM,), jnp.float32, -s, s)
        W2 = jax.random.uniform(ks[6], (DIM, DIM), jnp.float32, -s, s)
        b2 = jax.random.uniform(ks[7], (DIM,), jnp.float32, -s, s)
        return {'x': x, 'edge_index': edge_index, 'edge_weight': edge_weight, 'W1': W1, 'b1': b1, 'W2': W2, 'b2': b2}
    _L1_gnn_all = _L1_gnn_setup()
    _L1_gnn_in = {k: v for k, v in _L1_gnn_all.items() if k in ('W1', 'b1', 'W2', 'b2')}
    del _L1_gnn_all
    return {'x': x, 'src': src, 'dst': dst, 'edge_type_3': edge_type_3, 'edge_weight1': edge_weight1, 'L0_gnn_Wq': _L0_gnn_in['Wq'], 'L0_gnn_bq': _L0_gnn_in['bq'], 'L0_gnn_Wk': _L0_gnn_in['Wk'], 'L0_gnn_bk': _L0_gnn_in['bk'], 'L0_gnn_Wv': _L0_gnn_in['Wv'], 'L0_gnn_bv': _L0_gnn_in['bv'], 'L0_gnn_edge_emb': _L0_gnn_in['edge_emb'], 'L0_gnn_Wo': _L0_gnn_in['Wo'], 'L0_gnn_bo': _L0_gnn_in['bo'], 'L1_gnn_W1': _L1_gnn_in['W1'], 'L1_gnn_b1': _L1_gnn_in['b1'], 'L1_gnn_W2': _L1_gnn_in['W2'], 'L1_gnn_b2': _L1_gnn_in['b2']}

def reference(x, src, dst, edge_type_3, edge_weight1, L0_gnn_Wq, L0_gnn_bq, L0_gnn_Wk, L0_gnn_bk, L0_gnn_Wv, L0_gnn_bv, L0_gnn_edge_emb, L0_gnn_Wo, L0_gnn_bo, L1_gnn_W1, L1_gnn_b1, L1_gnn_W2, L1_gnn_b2):
    import jax
    import jax.numpy as jnp

    def _L0_gnn_ref(node_features, edges, edge_types, Wq, bq, Wk, bk, Wv, bv, edge_emb, Wo, bo):
        import jax, jax.numpy as jnp
        import numpy as np
        N_NODES = 6250
        N_EDGES = 37500
        INPUT_DIM = 128
        HIDDEN_DIM = 256
        NUM_HEADS = 8
        HEAD_DIM = HIDDEN_DIM // NUM_HEADS
        NUM_EDGE_TYPES = 3
        Q = (node_features @ Wq.T + bq).reshape(-1, NUM_HEADS, HEAD_DIM)
        K = (node_features @ Wk.T + bk).reshape(-1, NUM_HEADS, HEAD_DIM)
        V = (node_features @ Wv.T + bv).reshape(-1, NUM_HEADS, HEAD_DIM)
        src = edges[:, 0]
        tgt = edges[:, 1]
        scale = 1.0 / jnp.sqrt(jnp.float32(HEAD_DIM))
        scores = jnp.einsum('ehd,egd->ehg', Q[src], K[tgt]) * scale
        attn = jax.nn.softmax(scores, axis=-1)
        msg = jnp.einsum('ehg,egd->ehd', attn, V[tgt]).reshape(-1, HIDDEN_DIM)
        msg = msg + edge_emb[edge_types]
        out_e = msg @ Wo.T + bo
        messages = jax.ops.segment_sum(out_e, src, num_segments=N_NODES)
        return messages

    def _L1_gnn_ref(x, edge_index, edge_weight, W1, b1, W2, b2):
        import jax, jax.numpy as jnp
        import numpy as np
        N_NODES = 12500
        N_EDGES = 200000
        DIM = 128

        def _gcn_layer(x, row, col, ew, W, b):
            n = x.shape[0]
            h = x @ W.T + b
            ones = jnp.ones_like(ew)
            deg = jax.ops.segment_sum(ones, col, num_segments=n)
            dinv = jnp.where(deg > 0, deg ** (-0.5), 0.0)
            norm = dinv[row] * ew * dinv[col]
            msgs = norm[:, None] * h[row]
            return jax.ops.segment_sum(msgs, col, num_segments=n)
        n = x.shape[0]
        loop = jnp.arange(n, dtype=edge_index.dtype)
        row = jnp.concatenate([edge_index[0], loop])
        col = jnp.concatenate([edge_index[1], loop])
        ew = jnp.concatenate([edge_weight[:, 0], jnp.ones((n,), x.dtype)])
        h = _gcn_layer(x, row, col, ew, W1, b1)
        h = jax.nn.relu(h)
        h = _gcn_layer(h, row, col, ew, W2, b2)
        return jax.nn.sigmoid(h)
    edge_index = jnp.stack([src, dst])
    edge_index_t = jnp.stack([src, dst], axis=1)
    x = _layernorm(x + _L0_gnn_ref(x, edge_index_t, edge_type_3, L0_gnn_Wq, L0_gnn_bq, L0_gnn_Wk, L0_gnn_bk, L0_gnn_Wv, L0_gnn_bv, L0_gnn_edge_emb, L0_gnn_Wo, L0_gnn_bo), axis=-1)
    x = _layernorm(x + _L1_gnn_ref(x, edge_index, edge_weight1, L1_gnn_W1, L1_gnn_b1, L1_gnn_W2, L1_gnn_b2), axis=-1)
    return x

_drawn_inputs = setup_inputs


def setup_inputs(seed=0):
    import zlib

    import numpy as np

    out = dict(_drawn_inputs(seed))
    spreads = {}
    factors = {'edge_weight1': 26.29,
     'L0_gnn_bq': 5.534,
     'L0_gnn_bk': 5.178,
     'L1_gnn_W1': 4.939,
     'L1_gnn_b1': 8.0,
     'L1_gnn_W2': 3.591,
     'L1_gnn_b2': 8.0}
    for name, (base, spread) in spreads.items():
        noise = np.random.default_rng([zlib.crc32(name.encode()), seed]).standard_normal(out[name].shape)
        drawn = base * np.exp(spread * noise) if base else spread * noise
        out[name] = jnp.asarray(drawn.astype(out[name].dtype))
    for name, factor in factors.items():
        out[name] = (out[name] * factor).astype(out[name].dtype)
    return out
```

```python
import concourse.bass as bass
from concourse import mybir
from contextlib import ExitStack

F32, I32, BF16 = mybir.dt.float32, mybir.dt.int32, mybir.dt.bfloat16
ALU = mybir.AluOpType
ACT = mybir.ActivationFunctionType
AX = mybir.AxisListType

P = 128
N = 6250
E = 206250
NB = 49
NP = NB * P
WIN = 8
NW = NP // WIN
HI, LO = 25, 32
GT = 16
T = -(-E // (P * GT)) * GT
NG = T // GT
TC = -(-T // P)
H, D, HD = 8, 32, 256
TYPES = 3
GS = 8
NTILE = -(-(E // P + NW + (T * P - E) // P + 1) // GS) * GS
NGS = NTILE // GS
MC = -(-NTILE // P)
AW = D + TYPES
GE = 8
BIG = 1.0e30
EPS = 1e-5
PAD_SRC, PAD_DST = N + 14, NP - 1
NCH = 7
NACC = 2 * NB + 1


class Steps:

    def __init__(self, eng, sem, base=0):
        self.eng, self.sem, self.base, self.n = eng, sem, base, 0

    def do(self, ins):
        self.n += 1
        ins.then_inc(self.sem, 1)
        return self.n

    def need(self, n):
        self.eng.wait_ge(self.sem, self.base + n)

    def link(self, ins):
        self.need(self.do(ins))


def gnn_kernel(nc, x, src, dst, etype, ew, Wq, bq, Wk, bk, Wv, bv, emb, Wo, bo, W1, b1, W2, b2, out, dbg=None, stop=99):
    ctx = ExitStack()
    with ctx:
        def sb(name, shape, dt=F32):
            return ctx.enter_context(nc.sbuf_tensor(name, shape, dt))

        def sem(name):
            return ctx.enter_context(nc.semaphore(name))

        def dram(name, shape, dt=F32):
            return nc.dram_tensor(name, shape, dt).ap()

        def ge(eng, s, v):
            if not isinstance(v, int) or v > 0:
                eng.wait_ge(s, v)

        xpad2 = dram("xpad", (NP + P, P))
        xpad = xpad2[0:NP, :]
        kv_tab = dram("kv_tab", (NP, 2 * HD))
        qt_tab = dram("qt_tab", (NW, P, WIN * H))
        win_row = dram("win_row", (TC * P * P,))
        hi_row = dram("hi_row", (TC * P * P,))
        recs = dram("recs", (NTILE * P, 4), I32)
        start_row = dram("start_row", (HI * LO,))
        map_row = dram("map_row", (P * MC,), I32)
        msg_tab = dram("msg_tab", (NP, HD))
        cnt_tab = dram("cnt_tab", (NP, TYPES))
        x1_tab = dram("x1_tab", (NP, P))
        h_tab = [dram("h1_tab", (NP, P)), dram("h2_tab", (NP, P))]
        min_row = dram("min_row", (TC * P,))
        outpad = dram("outpad", (NP, P))

        ident = sb("ident", [P, P])
        identb = sb("identb", [P, P], BF16)
        iota_i = sb("iota_i", [P, P], I32)
        iota = sb("iota", [P, P])
        pcol = sb("pcol", [P, 1])
        pcol_i = sb("pcol_i", [P, 1], I32)
        npcol = sb("npcol", [P, 1])
        tri = sb("tri", [P, P])
        triT = sb("triT", [P, P])
        eps_c = sb("eps_c", [P, 1])
        zero_b = sb("zero_b", [P, LO], BF16)

        wqkvT = sb("wqkvT", [P, 3, HD])
        woT = sb("woT", [P, 2, P])
        w12T = sb("w12T", [P, 2, P])
        embT = sb("embT", [P, 2, TYPES])
        ebo = sb("ebo", [TYPES, P])
        b12 = sb("b12", [P, 2, P])

        dstT = sb("dstT", [P, TC * P])
        wT = sb("wT", [P, TC * P])
        sortbuf = sb("sortbuf", [P, 6 * TC * P])
        localT, typeT, winT, loT, hiT = (sortbuf[:, k * TC * P:(k + 1) * TC * P] for k in range(5))
        tmpT = sortbuf[:, 5 * TC * P:].bitcast(I32)
        srcI = sb("srcI", [P, TC * P], I32)
        dinv = sb("dinv", [P, NB])
        mapsb = sb("mapsb", [1, P * MC], I32)

        arena = sb("arena", [P, NW * AW])

        def carve(at, n, dt=F32):
            return arena[:, at:at + n] if dt is F32 else arena[:, at:at + n].bitcast(dt)

        raw = carve(0, 4 * TC * P, I32).rearrange("p (a c e) -> p a c e", a=4, c=TC)
        rawf = carve(4 * TC * P, 4 * TC * P).rearrange("p (a c e) -> p a c e", a=4, c=TC)
        digs = carve(8 * TC * P, 2 * TC * P, I32).rearrange("p (a c) -> p a c", a=2)
        hif = carve(10 * TC * P, TC * P).rearrange("p (c e) -> p c e", c=TC)
        span = sb("span", [P, 2 * TC])
        widest = sb("widest", [P, 1])
        wraw = sb("wraw", [P, 12, P])
        psum = ctx.enter_context(nc.psum_tensor("psum", [P, 8 * 512], F32))
        PS = [psum[:, 512 * i:512 * (i + 1)] for i in range(8)]
        SB = [psum[:, 0:1024], psum[:, 1024:2048]]
        PSM = PS[7].bitcast(BF16)
        FULL = E // P
        REST = E - FULL * P
        LC = TC - 1
        LROWS = FULL - LC * P

        s_c = sem("s_const")
        s_ld = sem("s_loaded")
        s_wl = sem("s_weights_loaded")
        s_rawf = sem("s_rawf")
        s_tp = sem("s_transposed")
        s_tc = sem("s_transposed_copied")
        s_d1 = sem("s_dve1")
        s_pad = sem("s_pad")
        s_dr = sem("s_rows_stored")
        s_embT = sem("s_embT")
        s_ebo = sem("s_ebo_ready")
        s_zp = sem("s_zero_pad")
        s_mm = sem("s_least_targets")

        with nc.Block() as block:
            @block.gpsimd
            def _(pool):
                st = Steps(pool, s_c)
                st.do(nc.gpsimd.memset(ident[:], 0.0))
                st.do(nc.gpsimd.memset(tri[:], 1.0))
                st.do(nc.gpsimd.memset(triT[:], 1.0))
                st.do(nc.gpsimd.memset(eps_c[:], EPS))
                st.do(nc.gpsimd.memset(zero_b[:], 0.0))
                st.do(nc.gpsimd.iota(iota_i[:], pattern=[[1, P]], base=0, channel_multiplier=0))
                st.link(nc.gpsimd.iota(pcol_i[:], pattern=[[0, 1]], base=0, channel_multiplier=1))
                st.do(nc.gpsimd.affine_select(out=ident[:], in_=ident[:], compare_op=ALU.not_equal, fill=1.0,
                                              base=0, pattern=[[-1, P]], channel_multiplier=1))
                st.do(nc.gpsimd.affine_select(out=tri[:], in_=tri[:], compare_op=ALU.is_gt, fill=0.0,
                                              base=0, pattern=[[-1, P]], channel_multiplier=1))
                st.do(nc.gpsimd.affine_select(out=triT[:], in_=triT[:], compare_op=ALU.is_gt, fill=0.0,
                                              base=0, pattern=[[1, P]], channel_multiplier=-1))
                st.do(nc.gpsimd.tensor_copy(iota[:], iota_i[:]))
                st.link(nc.gpsimd.tensor_copy(pcol[:], pcol_i[:]))
                st.do(nc.gpsimd.tensor_scalar(npcol[:], pcol[:], -1.0, None, ALU.mult))
                st.do(nc.gpsimd.tensor_copy(identb[:], ident[:]))

            NCONST = 14

            @block.sync
            def _(sp):
                for a, (v, dt) in enumerate(((src, I32), (dst, I32), (etype, I32), (ew, F32))):
                    to = raw[:, a] if dt is I32 else rawf[:, a]
                    sp.dma_start(to[:, 0:LC, :], v[0:LC * P * P].rearrange("(c t e) -> t c e", t=P, e=P)).then_inc(s_ld, 16)
                    if a == 0:
                        sp.wait_ge(s_pad, 4)
                    sp.dma_start(to[0:LROWS, LC, :],
                                 v[LC * P * P:FULL * P].rearrange("(t e) -> t e", e=P)).then_inc(s_ld, 16)
                    sp.dma_start(to[LROWS:LROWS + 1, LC, 0:REST],
                                 v[FULL * P:E].rearrange("(t e) -> t e", t=1)).then_inc(s_ld, 16)
                sp.wait_ge(s_rawf, 2)
                sp.dma_start(win_row.rearrange("(c t e) -> t c e", t=P, e=P), rawf[:, 0]).then_inc(s_dr, 16)
                sp.wait_ge(s_rawf, 4)
                sp.dma_start(hi_row.rearrange("(c t e) -> t c e", t=P, e=P), hif).then_inc(s_dr, 16)
                sp.wait_ge(s_mm, 1)
                sp.dma_start(min_row.rearrange("(c t) -> t c", t=P), span[:, 0:TC], allow_slow_non_contiguous=True).then_inc(s_dr, 16)
                sp.wait_ge(s_dr, 48)

            @block.scalar
            def _(act):
                for i, w in enumerate((Wq, Wk, Wv)):
                    act.dma_start(wraw[:, 2 * i:2 * i + 2, :], w.rearrange("(a p) f -> p a f", p=P)).then_inc(s_wl, 16)
                act.dma_start(wraw[:, 6:8, :], Wo.rearrange("o (a f) -> o a f", f=P)).then_inc(s_wl, 16)
                act.dma_start(wraw[:, 8, :], W1).then_inc(s_wl, 16)
                act.dma_start(wraw[:, 9, :], W2).then_inc(s_wl, 16)
                act.dma_start(wraw[0:TYPES, 10:12, :], emb.rearrange("t (a f) -> t a f", f=P)).then_inc(s_wl, 16)
                act.dma_start(b12[:, 0, :], bcast_rows(b1, P, P)).then_inc(s_wl, 16)
                act.dma_start(b12[:, 1, :], bcast_rows(b2, P, P)).then_inc(s_wl, 16)
                act.dma_start(ebo[:], bcast_rows(bo, TYPES, P)).then_inc(s_wl, 16)
                act.dma_start(xpad2[0:N, :], x).then_inc(s_wl, 16)
                act.wait_ge(s_zp, 1)
                act.dma_start(xpad2[N:NP, :], tmpT[0:NP - N, 0:P].bitcast(F32)).then_inc(s_wl, 16)
                act.dma_start(xpad2[NP:, :], tmpT[:, 0:P].bitcast(F32)).then_inc(s_wl, 16)
                act.wait_ge(s_wl, 13 * 16)

            @block.vector
            def _(dve):
                st = Steps(dve, s_d1)
                nc.vector.memset(raw[:, 0, LC, :], PAD_SRC).then_inc(s_pad, 1)
                nc.vector.memset(raw[:, 1, LC, :], PAD_DST).then_inc(s_pad, 1)
                nc.vector.memset(raw[:, 2, LC, :], 0).then_inc(s_pad, 1)
                nc.vector.memset(rawf[:, 3, LC, :], 0.0).then_inc(s_pad, 1)
                nc.vector.memset(tmpT, 0).then_inc(s_zp, 1)
                dve.wait_ge(s_ld, 12 * 16)
                st.link(nc.vector.tensor_scalar(digs[:, 0, :], raw[:, 0].rearrange("p c e -> p (c e)"), 3, None,
                                                ALU.arith_shift_right))
                nc.vector.tensor_copy(rawf[:, 0].rearrange("p c e -> p (c e)"), digs[:, 0, :]).then_inc(s_rawf, 1)
                dve.wait_ge(s_rawf, 1)
                st.link(nc.vector.tensor_copy(rawf[:, 1], raw[:, 1]))
                nc.vector.tensor_copy(rawf[:, 2], raw[:, 2]).then_inc(s_rawf, 1)
                dve.wait_ge(s_rawf, 2)
                st.link(nc.vector.tensor_scalar(digs[:, 1, :], raw[:, 0].rearrange("p c e -> p (c e)"), 7, None,
                                                ALU.bitwise_and))
                nc.vector.tensor_copy(raw[:, 0].bitcast(F32).rearrange("p c e -> p (c e)"), digs[:, 1, :]).then_inc(s_rawf, 1)
                st.link(nc.vector.tensor_scalar(digs[:, 0, :], digs[:, 0, :], 5, None, ALU.arith_shift_right))
                nc.vector.tensor_copy(hif.rearrange("p c e -> p (c e)"), digs[:, 0, :]).then_inc(s_rawf, 1)
                n = 0
                for target in (winT, dstT, typeT, wT, localT):
                    for c in range(0, TC, 4):
                        k = min(4, TC - c)
                        dve.wait_ge(s_tp, n + 1)
                        nc.vector.tensor_copy(target[:, c * P:(c + k) * P], PS[n % 4][:, 0:k * P]).then_inc(s_tc, 1)
                        n += 1
                nT = n
                for g in range(3):
                    dve.wait_ge(s_tp, n + 1)
                    n += 1
                    if g == 0:
                        nc.vector.tensor_copy(wqkvT[:].rearrange("p a f -> p (a f)")[:, 0:512], PS[(n - 1) % 4][:, :]).then_inc(s_tc, 1)
                    elif g == 1:
                        nc.vector.tensor_copy(wqkvT[:, 2, :], PS[(n - 1) % 4][:, 0:256]).then_inc(s_embT, 1)
                        nc.vector.tensor_copy(woT[:].rearrange("p a f -> p (a f)"), PS[(n - 1) % 4][:, 256:512]).then_inc(s_tc, 1)
                    else:
                        nc.vector.tensor_copy(w12T[:].rearrange("p a f -> p (a f)"), PS[(n - 1) % 4][:, 0:256]).then_inc(s_embT, 1)
                        nc.vector.tensor_copy(embT[:], PS[(n - 1) % 4][:, 256:512].rearrange("p (a t) -> p a t", a=2)[:, :, 0:TYPES]).then_inc(s_tc, 1)
                dve.wait_ge(s_wl, 13 * 16)
                dve.wait_ge(s_ebo, 1)
                st.link(nc.vector.tensor_tensor(ebo[:], PS[4][0:TYPES, 0:P], ebo[:], ALU.add))
                dve.wait_ge(s_tc, nT + 3)
                st.link(nc.vector.tensor_copy(tmpT[:], winT[:]))
                st.link(nc.vector.tensor_scalar(digs[:, 0, :], tmpT[:], 5, None, ALU.arith_shift_right))
                st.do(nc.vector.tensor_copy(hiT[:], digs[:, 0, :]))
                st.link(nc.vector.tensor_scalar(digs[:, 1, :], tmpT[:], 31, None, ALU.bitwise_and))
                st.link(nc.vector.tensor_copy(loT[:], digs[:, 1, :]))
                lo_c, hi_c = span[:, 0:TC], span[:, TC:2 * TC]
                nc.vector.tensor_reduce(lo_c, rawf[:, 1], AX.X, ALU.min).then_inc(s_mm, 1)
                dve.wait_ge(s_mm, 1)
                st.link(nc.vector.tensor_reduce(hi_c, rawf[:, 1], AX.X, ALU.max))
                st.link(nc.vector.tensor_tensor(hi_c, hi_c, lo_c, ALU.subtract))
                st.link(nc.vector.tensor_reduce(widest[:], hi_c, AX.X, ALU.max))

            @block.tensor
            def _(pe):
                pe.wait_ge(s_c, NCONST)
                n = 0
                for a in (0, 1, 2, 3, "local"):
                    pe.wait_ge(s_rawf, 3 if a == "local" else 2)
                    if a == 3:
                        pe.wait_ge(s_ld, 12 * 16)
                    for c in range(0, TC, 4):
                        if n >= 4:
                            pe.wait_ge(s_tc, n - 3)
                        for k in range(min(4, TC - c)):
                            frm = raw[:, 0].bitcast(F32)[:, c + k, :] if a == "local" else rawf[:, a, c + k, :]
                            last = nc.tensor.transpose(PS[n % 4][:, k * P:(k + 1) * P], frm, ident[:])
                        last.then_inc(s_tp, 1)
                        n += 1
                pe.wait_ge(s_wl, 13 * 16)
                for g in range(3):
                    pe.wait_ge(s_tc, n - 3)
                    for k in range(4):
                        i = 4 * g + k
                        if i < 10:
                            last = nc.tensor.transpose(PS[n % 4][:, k * P:(k + 1) * P], wraw[:, i, :], ident[:])
                        else:
                            last = nc.tensor.transpose(PS[n % 4][:, k * P:k * P + TYPES], wraw[0:TYPES, i, :], ident[0:TYPES, 0:TYPES])
                    last.then_inc(s_tp, 1)
                    n += 1
                pe.wait_ge(s_tc, n)
                pe.wait_ge(s_embT, 2)
                nc.tensor.matmul(PS[4][0:TYPES, 0:P], embT[:, 0, :], woT[:, 0, :], start=True, stop=False)
                nc.tensor.matmul(PS[4][0:TYPES, 0:P], embT[:, 1, :], woT[:, 1, :], start=False, stop=True).then_inc(s_ebo, 1)

        if stop == 1:
            dump(nc, ctx, dbg, [winT[:, 0:1616], localT[:, 0:1616], dstT[:, 0:1616], wT[:, 0:1616], ebo[:], widest[:]])
            return

        kvb = sb("kvb", [P, 2 * HD])
        bq4 = sb("bq4", [H, 4, D])
        bqT = sb("bqT", [P, H])
        wq4 = carve(0, H * P).rearrange("p (h r d) -> p h r d", h=H, r=4)
        xt_in = carve(1024, P)
        xT = carve(1280, P)
        kv_out = carve(1408, 2 * HD)
        qt_out = carve(1920, P * H)
        ohlo = [carve(3072 + 256 * i, 256, BF16).rearrange("p (t d) -> p t d", t=GT) for i in range(2)]
        ohhi = [carve(3584 + 256 * i, 200, BF16).rearrange("p (t d) -> p t d", t=GT) for i in range(2)]
        prefill = carve(4096, 2400, I32)
        startb = carve(6500, NW)
        junk = carve(7300, NW)
        tau_i = carve(8100, MC, I32)
        tau = carve(8120, MC)
        mapf = carve(8140, MC)
        map_i = carve(8160, MC, I32)
        ntile_i = carve(8200, LO, I32)
        ntile = carve(8240, LO)
        incl = carve(8280, LO)
        ones_r = carve(8320, LO)
        start = carve(8360, LO)
        carry = sb("carry", [HI, LO])
        rowmax = carve(8400, P)
        passes = sb("passes", [1, 1], I32)

        s_k2 = sem("s_kvq_consts")
        s_b2 = sem("s_biases_loaded")
        s_bqp = sem("s_bq_transposed")
        s_bqc = sem("s_bq_copied")
        s_xin = sem("s_x_in")
        s_xp = sem("s_x_transposed")
        s_xc = sem("s_xT_copied")
        s_kvp = sem("s_kv_product")
        s_kvc = sem("s_kv_biased")
        s_qp = sem("s_q_product")
        s_qc = sem("s_q_biased")
        s_kvs = sem("s_kv_stored")
        s_qs = sem("s_q_stored")
        s_oh = sem("s_onehots")
        s_cn = sem("s_counted")
        s_hb = sem("s_hi_base")
        s_p2 = sem("s_prefix")
        s_st = sem("s_starts_stored")
        s_stb = sem("s_starts_back")
        s_map = sem("s_map")
        s_maps = sem("s_map_stored")
        s_rp = sem("s_prefill")
        s_rps = sem("s_prefilled")
        s_tau = sem("s_tau")
        s_wm = sem("s_widest_row")

        with nc.Block() as block:
            @block.sync
            def _(sp):
                sp.dma_start(kvb[:, 0:HD], bcast_rows(bk, P, HD)).then_inc(s_b2, 16)
                sp.dma_start(kvb[:, HD:], bcast_rows(bv, P, HD)).then_inc(s_b2, 16)
                for r in range(4):
                    sp.dma_start(bq4[:, r, :], bq.rearrange("(h d) -> h d", h=H)).then_inc(s_b2, 16)
                sp.dma_start(xt_in, xpad[0:P, :]).then_inc(s_xin, 16)
                sp.wait_ge(s_rp, 4)
                for k in range(4):
                    r = NTILE * P // 4
                    sp.dma_start(recs[k * r:(k + 1) * r, :].rearrange("(p r) w -> p (r w)", p=P), prefill).then_inc(s_rps, 16)

                xnext = xpad2[P:P + NP, :]
                def body(i):
                    sp.wait_ge(s_xp, i + 1)
                    sp.dma_start(xt_in, xnext[bass.ds(i * P, P), :]).then_inc(s_xin, 16)
                    sp.wait_ge(s_kvc, i + 1)
                    sp.dma_start(kv_tab[bass.ds(i * P, P), :], kv_out).then_inc(s_kvs, 16)
                    sp.wait_ge(s_qc, i * H + H)
                    sp.dma_start(qt_tab[bass.ds(i * GT, GT), :, :].rearrange("w p c -> p w c"),
                                 qt_out.rearrange("p (w c) -> p w c", w=GT)).then_inc(s_qs, 16)
                body(0)
                with sp.Fori(1, NB) as i:
                    body(i)
                sp.wait_ge(s_xin, 16 * (NB + 1))
                sp.wait_ge(s_kvs, 16 * NB)
                sp.wait_ge(s_qs, 16 * NB)
                sp.wait_ge(s_p2, 6)
                sp.dma_start(start_row.rearrange("(h l) -> h l", h=HI), start[0:HI, :]).then_inc(s_st, 16)
                sp.wait_ge(s_st, 16)
                sp.dma_start(startb, bcast_rows(start_row, P, NW)).then_inc(s_stb, 16)
                sp.wait_ge(s_map, MC + 2)
                sp.dma_start(map_row.rearrange("(p c) -> p c", p=P), map_i).then_inc(s_maps, 16)
                sp.wait_ge(s_maps, 16)
                sp.dma_start(mapsb[:], map_row.unsqueeze(0)).then_inc(s_maps, 16)
                sp.wait_ge(s_maps, 32)
                sp.wait_ge(s_rps, 64)

            @block.gpsimd
            def _(pool):
                rp = Steps(pool, s_rp)
                v = prefill.rearrange("p (r w) -> p r w", w=4)
                rp.do(nc.gpsimd.memset(v[:, :, 0:1], 0))
                rp.do(nc.gpsimd.memset(v.bitcast(F32)[:, :, 1:3], -1.0))
                rp.do(nc.gpsimd.memset(v[:, :, 3:4], 0))
                rp.do(nc.gpsimd.memset(ones_r, 1.0))
                nc.gpsimd.iota(tau_i, pattern=[[1, MC]], base=0, channel_multiplier=MC).then_inc(s_tau, 1)
                pool.wait_ge(s_tau, 1)
                nc.gpsimd.tensor_copy(tau, tau_i).then_inc(s_tau, 1)

            @block.scalar
            def _(act):
                act.wait_ge(s_bqp, 1)
                nc.scalar.activation(bqT[:], PS[5][:, 0:H], ACT.Copy).then_inc(s_bqc, 1)
                act.wait_ge(s_bqc, 1)
                def body(i):
                    act.wait_ge(s_xp, i + 1)
                    nc.scalar.activation(xT, PS[0][:, 0:P], ACT.Copy).then_inc(s_xc, 1)
                    act.wait_ge(s_qp, i + 1)
                    ge(act, s_qs, i * 16)
                    to = qt_out.rearrange("p (n h) -> p n h", h=H)
                    for h in range(H):
                        nc.scalar.activation(to[:, :, h], PS[2 + h // 4][:, (h % 4) * P:(h % 4 + 1) * P], ACT.Identity,
                                             bias=bqT[:, h:h + 1]).then_inc(s_qc, 1)
                body(0)
                with act.Fori(1, NB) as i:
                    body(i)

            @block.vector
            def _(dve):
                nc.vector.tensor_copy(wq4, wqkvT[:, 0, :].rearrange("p (h d) -> p h d", h=H).unsqueeze(2)
                                      .to_broadcast([P, H, 4, D])).then_inc(s_k2, 1)
                dve.wait_ge(s_b2, 6 * 16)
                def kv_bias(i):
                    dve.wait_ge(s_kvp, i + 1)
                    ge(dve, s_kvs, i * 16)
                    nc.vector.tensor_tensor(kv_out, PS[1][:, :], kvb[:], ALU.add).then_inc(s_kvc, 1)
                kv_bias(0)
                with dve.Fori(1, NB) as i:
                    kv_bias(i)
                def onehots(g, b):
                    at = bass.ds(g * GT, GT)
                    nc.vector.tensor_tensor(ohlo[b], loT[:, at].unsqueeze(2).to_broadcast([P, GT, LO]),
                                            iota[:, 0:LO].unsqueeze(1).to_broadcast([P, GT, LO]), ALU.is_equal).then_inc(s_oh, 1)
                    nc.vector.tensor_tensor(ohhi[b], hiT[:, at].unsqueeze(2).to_broadcast([P, GT, HI]),
                                            iota[:, 0:HI].unsqueeze(1).to_broadcast([P, GT, HI]), ALU.is_equal).then_inc(s_oh, 1)
                onehots(0, 0)

                def two_groups(i):
                    ge(dve, s_cn, i * 2)
                    onehots(i * 2 + 1, 1)
                    dve.wait_ge(s_cn, i * 2 + 1)
                    onehots(i * 2 + 2, 0)
                two_groups(0)
                with dve.Fori(1, NG // 2) as i:
                    two_groups(i)
                st = Steps(dve, s_p2)
                dve.wait_ge(s_cn, NG + 1)
                dve.wait_ge(s_rp, 4)
                st.link(nc.vector.tensor_scalar(ntile_i[0:HI, :], PS[4][0:HI, 0:LO], float(P - 1), None, ALU.add))
                st.link(nc.vector.tensor_scalar(ntile_i[0:HI, :], ntile_i[0:HI, :], 7, None, ALU.arith_shift_right))
                st.link(nc.vector.tensor_copy(ntile[0:HI, :], ntile_i[0:HI, :]))
                st.link(nc.vector.tensor_tensor_scan(incl[0:HI, :], ones_r[0:HI, :], ntile[0:HI, :], 0.0, ALU.mult, ALU.add))
                st.link(nc.vector.tensor_tensor(start[0:HI, :], incl[0:HI, :], ntile[0:HI, :], ALU.subtract))
                dve.wait_ge(s_hb, 1)
                st.link(nc.vector.tensor_scalar(start[0:HI, :], start[0:HI, :], PS[5][0:HI, 64:65], None, ALU.add))
                st.link(nc.vector.tensor_scalar(carry[:], start[0:HI, :], float(P), None, ALU.mult))
                dve.wait_ge(s_wm, 1)
                st.link(nc.vector.tensor_reduce(rowmax[0:1, 0:1], PS[6][0:1, 0:P], AX.X, ALU.max))
                st.link(nc.vector.tensor_scalar(passes[:], rowmax[0:1, 0:1], float(P), None, ALU.add))
                st.link(nc.vector.tensor_scalar(passes[:], passes[:], 7, None, ALU.arith_shift_right))
                dve.wait_ge(s_stb, 16)
                dve.wait_ge(s_tau, 2)
                mp = Steps(dve, s_map)
                for c in range(MC):
                    mp.link(nc.vector.tensor_scalar(junk, startb, tau[:, c:c + 1], 0.0, ALU.is_le, ALU.add,
                                                    accum_out=mapf[:, c:c + 1]))
                mp.link(nc.vector.tensor_scalar(mapf, mapf, -1.0, None, ALU.add))
                mp.link(nc.vector.tensor_copy(map_i, mapf))

            @block.tensor
            def _(pe):
                pe.wait_ge(s_b2, 6 * 16)
                nc.tensor.transpose(PS[5][:, 0:H], bq4[:].rearrange("h r d -> h (r d)"), ident[0:H, 0:H]).then_inc(s_bqp, 1)
                nc.tensor.transpose(PS[6][0:1, 0:P], widest[:], ident[:]).then_inc(s_wm, 1)
                pe.wait_ge(s_k2, 1)

                def body(i):
                    pe.wait_ge(s_xin, i * 16 + 16)
                    ge(pe, s_xc, i)
                    nc.tensor.transpose(PS[0][:, 0:P], xt_in, ident[:]).then_inc(s_xp, 1)
                    pe.wait_ge(s_xc, i + 1)
                    ge(pe, s_kvc, i)
                    nc.tensor.matmul(PS[1][:, :], xT, wqkvT[:, 1:3, :].rearrange("p a f -> p (a f)"), start=True, stop=True).then_inc(s_kvp, 1)
                    ge(pe, s_qc, i * H)
                    for h in range(H):
                        last = nc.tensor.matmul(PS[2 + h // 4][:, (h % 4) * P:(h % 4 + 1) * P],
                                                wq4[:, h].rearrange("p r d -> p (r d)"), xT, start=True, stop=True)
                    last.then_inc(s_qp, 1)
                body(0)
                with pe.Fori(1, NB) as i:
                    body(i)
                nc.tensor.matmul(PS[4][0:HI, 0:LO], zero_b[:, 0:HI], zero_b[:, 0:LO], start=True, stop=False)

                def count(g, b):
                    pe.wait_ge(s_oh, g * 2 + 2)
                    for t in range(GT):
                        last = nc.tensor.matmul(PS[4][0:HI, 0:LO], ohhi[b][:, t, :], ohlo[b][:, t, :], start=False, stop=False)
                    last.then_inc(s_cn, 1)
                with pe.Fori(0, NG // 2) as i:
                    count(i * 2, 0)
                    count(i * 2 + 1, 1)
                count(NG - 1, 0)
                nc.tensor.matmul(PS[4][0:HI, 0:LO], zero_b[:, 0:HI], zero_b[:, 0:LO], start=False, stop=True).then_inc(s_cn, 1)
                pe.wait_ge(s_p2, 4)
                nc.tensor.matmul(PS[5][0:HI, 64:65], triT[0:HI, 0:HI], incl[0:HI, LO - 1:LO], start=True, stop=True).then_inc(s_hb, 1)

        if stop == 2:
            dump(nc, ctx, dbg, [carry[:], mapsb[:, 0:2048].bitcast(F32), passes[:].bitcast(F32)], [(kv_tab[1024:1152], 3), (qt_tab[767], 4)])
            return

        G2 = GT * P
        win_b = [carve(G2 * i, G2) for i in range(2)]
        hi_b = [carve(G2 * (2 + i), G2) for i in range(2)]
        hiT1 = [carve(G2 * (4 + i), G2) for i in range(2)]
        habs = carve(G2 * 6, G2)
        at = G2 * 7
        dlo_oh = [carve(at + 1024 * i, 1024, BF16).rearrange("p (t d) -> p t d", t=GT) for i in range(2)]
        dhi_oh = [carve(at + 2048 + 392 * i, 392, BF16).rearrange("p (t d) -> p t d", t=GT) for i in range(2)]
        at += 2048 + 784
        ohlo3 = [carve(at + 256 * i, 256, BF16).rearrange("p (t d) -> p t d", t=GT) for i in range(2)]
        ohhi3 = [carve(at + 512 + 200 * i, 200, BF16).rearrange("p (t d) -> p t d", t=GT) for i in range(2)]
        at += 912
        LG = GT + 1
        hin = carve(at, LO * LG).rearrange("p (l t) -> p l t", l=LO)
        keep = carve(at + LO * LG, LO * LG)
        base = [carve(at + (2 + i) * LO * LG, LO * LG).rearrange("p (l t) -> p l t", l=LO) for i in range(2)]
        at += 4 * LO * LG
        looked = carve(at, GT * LO).rearrange("p (t l) -> p t l", t=GT)
        at += GT * LO
        rank = [carve(at + GT * i, GT) for i in range(2)]
        place = carve(at + 2 * GT, GT)
        place_i, pa, pb_ = (carve(at + (3 + i) * GT, GT, I32) for i in range(3))
        addr = [carve(at + (6 + i) * GT, GT, I32) for i in range(2)]
        at += 8 * GT
        rec = [carve(at + 4 * GT * i, 4 * GT, I32).rearrange("p (t w) -> p t w", t=GT) for i in range(2)]
        at += 8 * GT
        same = carve(at, P)
        dhiT = carve(at + P, TC * P)
        dig_i = carve(at + P + TC * P, TC * P, I32)
        dhiT2 = carve(G2 * 7, TC * P)
        dloT = sb("dloT", [P, TC * P])

        s_wb = [sem(f"s_windows_row{i}") for i in range(2)]
        s_hb3 = [sem(f"s_hi_row{i}") for i in range(2)]
        s_ini = sem("s_sort_start")
        s_oh3 = sem("s_onehots3")
        s_hc = sem("s_tile_counts")
        s_h1 = sem("s_hi_onehotT")
        s_v3 = sem("s_sort_steps")
        s_lk = sem("s_bases_looked_up")
        s_dg = sem("s_degree_onehots")
        s_dgc = sem("s_degrees_counted")
        s_sc = [sem(f"s_scattered{i}") for i in range(2)]
        s_sq = sem("s_degree_roots")
        s_go = sem("s_pool_goes_on")
        KR, KS, KM, KA = GT, GT + 3, GT + 5, GT + 15

        with nc.Block() as block:
            @block.sync
            def _(sp):
                def group(g, u, b):
                    sp.wait_ge(s_v3, (g - 2) * KA + KR) if not isinstance(g, int) or g >= 2 else None
                    sp.dma_start(win_b[b], win_row[bass.ds(g * G2, G2)].unsqueeze(0).to_broadcast([P, G2])).then_inc(s_wb[b], 16)
                    sp.wait_ge(s_h1, (g - 2) * 2 + 1) if not isinstance(g, int) or g >= 2 else None
                    sp.dma_start(hi_b[b][0:HI], hi_row[bass.ds(g * G2, G2)].unsqueeze(0).to_broadcast([HI, G2])).then_inc(s_hb3[b], 16)
                group(0, 0, 0)
                group(1, 0, 1)
                with sp.Fori(1, NG // 2) as i:
                    group(i * 2, i, 0)
                    group(i * 2 + 1, i, 1)
                group(NG - 1, 0, 0)

            @block.gpsimd
            def _(pool):
                def group(g, b):
                    pool.wait_ge(s_v3, (g + 1) * KA)
                    pool.sem_inc(s_go, 1)
                    for t in range(GT):
                        nc.gpsimd.indirect_dma_start(recs, bass.IndirectOffsetOnAxis(ap=addr[b][:, t:t + 1], axis=0),
                                                     rec[b][:, t, :], None).then_inc(s_sc[b], 16)
                with pool.Fori(0, NG // 2) as i:
                    group(i * 2, 0)
                    group(i * 2 + 1, 1)
                group(NG - 1, 0)
                pool.wait_ge(s_sc[0], 16 * GT * (NG // 2 + 1))
                pool.wait_ge(s_sc[1], 16 * GT * (NG // 2))

            @block.scalar
            def _(act):
                def group(g, i, b):
                    act.wait_ge(s_hb3[b], i * 16 + 16)
                    ge(act, s_h1, g * 2)
                    nc.scalar.activation(habs[0:HI], hi_b[b][0:HI], ACT.Abs, bias=npcol[0:HI, :]).then_inc(s_h1, 1)
                    act.wait_ge(s_h1, g * 2 + 1)
                    if not isinstance(g, int) or g >= 2:
                        act.wait_ge(s_lk, g - 1)
                    nc.scalar.activation(hiT1[b][0:HI], habs[0:HI], ACT.Relu, bias=1.0, scale=-1.0).then_inc(s_h1, 1)
                group(0, 0, 0)
                group(1, 0, 1)
                with act.Fori(1, NG // 2) as i:
                    group(i * 2, i, 0)
                    group(i * 2 + 1, i, 1)
                group(NG - 1, NG // 2, 0)
                act.wait_ge(s_dgc, NG + 1)
                nc.scalar.activation(dinv[:], PS[2][:, 0:NB], ACT.Sqrt, bias=1.0).then_inc(s_sq, 1)

            @block.vector
            def _(dve):
                si = Steps(dve, s_ini)
                si.do(nc.vector.memset(rec[0], 0))
                si.do(nc.vector.memset(rec[1], 0))
                si.link(nc.vector.tensor_copy(tmpT[:], dstT[:]))
                si.link(nc.vector.tensor_scalar(dig_i, tmpT[:], 7, None, ALU.arith_shift_right))
                si.link(nc.vector.tensor_copy(dhiT, dig_i))
                si.link(nc.vector.tensor_scalar(dig_i, tmpT[:], P - 1, None, ALU.bitwise_and))
                si.link(nc.vector.tensor_copy(dloT[:], dig_i))
                si.link(nc.vector.tensor_scalar(dig_i, winT, float(WIN), None, ALU.mult))
                si.link(nc.vector.tensor_copy(dhiT2, dig_i))
                si.link(nc.vector.tensor_tensor(srcI[:], dhiT2, localT, ALU.add))
                si.do(nc.vector.memset(hin[0:HI], 0.0))
                si.link(nc.vector.memset(keep[0:HI], 1.0))
                si.link(nc.vector.memset(keep[0:HI].rearrange("p (l t) -> p l t", l=LO)[:, :, 0:1], 0.0))
                si.link(nc.vector.tensor_copy(base[1][0:HI, :, GT], carry[:]))

                def group(g, i, b):
                    st = Steps(dve, s_v3, g * KA)
                    col = bass.ds(g * GT, GT)
                    later = not isinstance(g, int) or g >= 2
                    if later:
                        dve.wait_ge(s_hc, g - 1)
                    nc.vector.tensor_tensor(ohlo3[b], loT[:, col].unsqueeze(2).to_broadcast([P, GT, LO]),
                                            iota[:, 0:LO].unsqueeze(1).to_broadcast([P, GT, LO]), ALU.is_equal).then_inc(s_oh3, 1)
                    nc.vector.tensor_tensor(ohhi3[b], hiT[:, col].unsqueeze(2).to_broadcast([P, GT, HI]),
                                            iota[:, 0:HI].unsqueeze(1).to_broadcast([P, GT, HI]), ALU.is_equal).then_inc(s_oh3, 1)
                    dve.wait_ge(s_wb[b], i * 16 + 16)
                    for t in range(GT):
                        if t:
                            st.need(t)
                        elif later or g == 1:
                            dve.wait_ge(s_v3, g * KA)
                        st.do(nc.vector.scalar_tensor_tensor(same, win_b[b][:, t * P:(t + 1) * P], winT[:, bass.ds(g * GT + t, 1)],
                                                             tri[:], ALU.is_equal, ALU.mult, accum_out=rank[b][:, t:t + 1]))
                    dve.wait_ge(s_hc, g + 1)
                    st.do(nc.vector.tensor_copy(hin[0:HI, :, 1:LG], PS[b][0:HI, :].rearrange("p (t l) -> p l t", l=LO)))
                    st.link(nc.vector.tensor_copy(hin[0:HI, :, 0], base[1 - b][0:HI, :, GT]))
                    if later:
                        dve.wait_ge(s_lk, g - 1)
                    assert st.n == KR + 2
                    st.do(nc.vector.tensor_tensor_scan(base[b][0:HI].rearrange("p l t -> p (l t)"), keep[0:HI],
                                                       hin[0:HI].rearrange("p l t -> p (l t)"), 0.0, ALU.mult, ALU.add))
                    assert st.n == KS
                    if later:
                        dve.wait_ge(s_dgc, g - 1)
                    nc.vector.tensor_tensor(dlo_oh[b], dloT[:, col].unsqueeze(2).to_broadcast([P, GT, P]),
                                            iota[:].unsqueeze(1).to_broadcast([P, GT, P]), ALU.is_equal).then_inc(s_dg, 1)
                    nc.vector.tensor_tensor(dhi_oh[b], dhiT[:, col].unsqueeze(2).to_broadcast([P, GT, NB]),
                                            iota[:, 0:NB].unsqueeze(1).to_broadcast([P, GT, NB]), ALU.is_equal).then_inc(s_dg, 1)
                    dve.wait_ge(s_lk, g + 1)
                    st.link(nc.vector.tensor_tensor(looked, PS[3 + b][:, :].rearrange("p (t l) -> p t l", t=GT), ohlo3[b], ALU.mult))
                    st.link(nc.vector.tensor_reduce(place, looked, AX.X, ALU.add))
                    assert st.n == KM
                    st.link(nc.vector.tensor_tensor(place, place, rank[b], ALU.add))
                    st.link(nc.vector.tensor_copy(place_i, place))
                    if later:
                        dve.wait_ge(s_sc[b], i * (16 * GT))
                    st.do(nc.vector.tensor_scalar(pa, place_i, 10, 10, ALU.arith_shift_right, ALU.logical_shift_left))
                    st.link(nc.vector.tensor_scalar(pb_, place_i, P - 1, 3, ALU.bitwise_and, ALU.logical_shift_left))
                    st.do(nc.vector.tensor_scalar(place_i, place_i, 7, GS - 1, ALU.arith_shift_right, ALU.bitwise_and))
                    st.link(nc.vector.tensor_tensor(pa, pa, pb_, ALU.bitwise_or))
                    st.do(nc.vector.tensor_copy(rec[b][:, :, 0], dstT[:, col]))
                    st.do(nc.vector.tensor_copy(rec[b][:, :, 1].bitcast(F32), localT[:, col]))
                    st.do(nc.vector.tensor_copy(rec[b][:, :, 2].bitcast(F32), typeT[:, col]))
                    st.link(nc.vector.tensor_tensor(addr[b], pa, place_i, ALU.bitwise_or))
                    assert st.n == KA, st.n
                group(0, 0, 0)
                group(1, 0, 1)
                with dve.Fori(1, NG // 2) as i:
                    group(i * 2, i, 0)
                    group(i * 2 + 1, i, 1)
                group(NG - 1, NG // 2, 0)
                dve.wait_ge(s_sq, 1)
                si.link(nc.vector.reciprocal(dinv[:], dinv[:]))

            @block.tensor
            def _(pe):
                pe.wait_ge(s_ini, 14)

                def group(g, b):
                    pe.wait_ge(s_oh3, g * 2 + 2)
                    if not isinstance(g, int) or g >= 2:
                        pe.wait_ge(s_v3, (g - 2) * KA + KR + 1)
                    for t in range(GT):
                        last = nc.tensor.matmul(PS[b][0:HI, t * LO:(t + 1) * LO], ohhi3[b][:, t, :], ohlo3[b][:, t, :], start=True, stop=True)
                    last.then_inc(s_hc, 1)
                    pe.wait_ge(s_h1, g * 2 + 2)
                    pe.wait_ge(s_v3, g * KA + KS)
                    for t in range(GT):
                        last = nc.tensor.matmul(PS[3 + b][:, t * LO:(t + 1) * LO], hiT1[b][0:HI, t * P:(t + 1) * P], base[b][0:HI, :, t], start=True, stop=True)
                    last.then_inc(s_lk, 1)
                    pe.wait_ge(s_dg, g * 2 + 2)
                    for t in range(GT):
                        last = nc.tensor.matmul(PS[2][:, 0:NB], dlo_oh[b][:, t, :], dhi_oh[b][:, t, :],
                                                start=isinstance(g, int) and g == 0 and t == 0, stop=False)
                    last.then_inc(s_dgc, 1)
                group(0, 0)
                group(1, 1)
                with pe.Fori(1, NG // 2) as i:
                    group(i * 2, 0)
                    group(i * 2 + 1, 1)
                group(NG - 1, 0)
                nc.tensor.matmul(PS[2][:, 0:LO], identb[:], zero_b[:], start=False, stop=True).then_inc(s_dgc, 1)

        if stop == 3:
            dump(nc, ctx, dbg, [dinv[:]], [(recs.rearrange("(p a) w -> p (a w)", p=P)[:, i * 2048:(i + 1) * 2048].bitcast(F32), 1 + i) for i in range(4)])
            return

        U = 2 * GS
        NBODY = NTILE // U
        NPAIR = NTILE // 2
        PAIRS = GS // 2
        C8 = WIN * H

        def spare(at, n, dt=F32):
            v = sortbuf[:, at:at + n]
            return v if dt is F32 else v.bitcast(dt)

        kv_in = [spare(512 * i, 512) for i in range(GS)]
        kT = [spare(4096 + 512 * i, 512) for i in range(2)]
        qt_in = [spare(5120 + 2 * C8 * i, 2 * C8).rearrange("p (t c) -> p t c", t=2) for i in range(PAIRS)]
        bq_ = [spare(5632 + 512 * i, 512).rearrange("p (t j c) -> p t j c", t=2, j=4) for i in range(2)]
        em = [spare(6656 + 1024 * i, 1024).rearrange("p (t g c) -> p t g c", t=2, g=H) for i in range(2)]
        ohpad = [spare(8704 + 512 * i, 512).rearrange("p (t c) -> p t c", t=GS) for i in range(2)]
        masksel = sb("masksel", [GS * WIN, GS * C8], BF16)
        gmask = sb("gmask", [P, 4])
        rec_in = [sb(f"rec_in{i}", [P, 4 * GS], I32) for i in range(2)]
        small = wraw[:].rearrange("p a f -> p (a f)")
        typ = [small[:, 24 * i:24 * i + 24].rearrange("p (t y) -> p t y", y=TYPES) for i in range(2)]
        nm = [small[:, 64 + 64 * i:128 + 64 * i].bitcast(BF16) for i in range(2)]
        nmT = [small[0:GS * WIN, 192 + 64 * i:256 + 64 * i].bitcast(BF16) for i in range(2)]
        sc = [small[:, 320 + 128 * i:448 + 128 * i] for i in range(2)]
        exs = [small[:, 576 + 128 * i:704 + 128 * i] for i in range(2)]
        top = sb("top", [P, 2 * H])
        den = sb("den", [P, 2 * H])
        tiny = sb("tiny", [1, 2])
        acc = arena[0:C8, :]

        s_k4 = sem("s_l0_consts")
        s_k4v = sem("s_l0_zeroed")
        s_rec = [sem(f"s_records_in{i}") for i in range(2)]
        s_qt = [sem(f"s_queries_in{i}") for i in range(PAIRS)]
        s_kv = [sem(f"s_gathered{i}") for i in range(GS)]
        s_bq = sem("s_q_spread")
        s_ktc = sem("s_kT_copied")
        s_kt = sem("s_k_transposed")
        s_s = sem("s_scores")
        s_pv = sem("s_values_summed")
        s_oh4 = sem("s_group_onehots")
        s_nmt = sem("s_mask_transposed")
        s_nmc = sem("s_mask_copied")
        s_v4 = sem("s_softmax_steps")
        s_ex = sem("s_exps")
        s_ms = sem("s_messages_stored")
        s_go4 = sem("s_pool_goes_on4")
        K4 = 10
        REDUCED, SHIFTED, ADDED, SPREAD = 1, 3, 5, 10

        with nc.Block() as block:
            @block.sync
            def _(sp):
                def body(i):
                    for q in range(U // 2):
                        g = i * (U // 2) + q
                        if q % PAIRS == 0:
                            grp = i * 2 + q // PAIRS
                            if not isinstance(i, int):
                                for t in range(GS):
                                    sp.wait_ge(s_kv[t], (grp - 1) * 16)
                                sp.wait_ge(s_oh4, grp - 1)
                            sp.dma_start(rec_in[q // PAIRS][:], recs[bass.ds(grp * (P * GS), P * GS), :]
                                         .rearrange("(p t) w -> p (t w)", p=P)).then_inc(s_rec[q // PAIRS], 16)
                        ws = [sp.value_load(mapsb[0:1, bass.ds(g * 2 + t, 1)], min_val=0, max_val=NW - 1) for t in range(2)]
                        ge(sp, s_bq, g - PAIRS + 1)
                        for t, w in enumerate(ws):
                            sp.dma_start(qt_in[q % PAIRS][:, t, :], qt_tab[bass.ds(w, 1), :, :].rearrange("w p c -> (w p) c")).then_inc(s_qt[q % PAIRS], 16)
                body(0)
                with sp.Fori(1, NBODY) as i:
                    body(i)
                sp.wait_ge(s_v4, NPAIR * K4 + 2)
                a3 = acc.rearrange("c (w a) -> c w a", a=AW)
                m3 = msg_tab.rearrange("(w s) (h d) -> (s h) w d", s=WIN, h=H)
                for k in range(4):
                    ws = slice(k * (NW // 4), (k + 1) * (NW // 4))
                    sp.dma_start(m3[:, ws, :], a3[:, ws, 0:D]).then_inc(s_ms, 16)
                sp.dma_start(cnt_tab.rearrange("(w s) t -> s w t", s=WIN), a3[0:WIN, :, D:AW]).then_inc(s_ms, 16)
                sp.wait_ge(s_ms, 80)

            @block.gpsimd
            def _(pool):
                ks = Steps(pool, s_k4)
                ks.link(nc.gpsimd.memset(masksel[:], -BIG))
                for t in range(GS):
                    vt = masksel[:, t * C8:(t + 1) * C8].rearrange("p (s h) -> p s h", s=WIN)
                    ks.do(nc.gpsimd.affine_select(out=vt, in_=vt, compare_op=ALU.is_equal, fill=0.0, base=-WIN * t,
                                                  pattern=[[-1, WIN], [0, H]], channel_multiplier=1))
                ks.link(nc.gpsimd.memset(gmask[:], 1.0))
                ks.link(nc.gpsimd.affine_select(out=gmask[:], in_=gmask[:], compare_op=ALU.is_ge, fill=0.0, base=0,
                                                pattern=[[-D, 4]], channel_multiplier=1))
                ks.link(nc.gpsimd.affine_select(out=gmask[:], in_=gmask[:], compare_op=ALU.is_ge, fill=0.0, base=D - 1,
                                                pattern=[[D, 4]], channel_multiplier=-1))

                def group(grp, b):
                    pool.wait_ge(s_rec[b], (grp - b) * 8 + 16)
                    pool.sem_inc(s_go4, 1)
                    for t in range(GS):
                        if t % 2 == 0:
                            ge(pool, s_pv, grp * PAIRS - PAIRS + t // 2 + 1)
                            pool.sem_inc(s_go4, 1)
                        nc.gpsimd.indirect_dma_start(kv_in[t], None, kv_tab,
                                                     bass.IndirectOffsetOnAxis(ap=rec_in[b][:, 4 * t:4 * t + 1], axis=0)).then_inc(s_kv[t], 16)
                group(0, 0)
                group(1, 1)
                with pool.Fori(1, NBODY) as i:
                    group(i * 2, 0)
                    group(i * 2 + 1, 1)

            @block.scalar
            def _(act):
                def spread(g, q, uses):
                    ge(act, s_s, g - 1)
                    act.wait_ge(s_qt[q % PAIRS], uses * 32)
                    for j in range(4):
                        last = nc.scalar.activation(bq_[q % 2][:, :, j, :], qt_in[q % PAIRS], ACT.Copy, scale=gmask[:, j:j + 1])
                    last.then_inc(s_bq, 1)
                    act.wait_ge(s_kt, g + 1)
                    nc.scalar.activation(kT[q % 2], PS[4][:, :], ACT.Copy).then_inc(s_ktc, 1)

                def mask(grp, b):
                    act.wait_ge(s_nmt, grp + 1)
                    ge(act, s_s, grp * PAIRS - PAIRS)
                    nc.scalar.activation(nmT[b], PSM[0:GS * WIN, 0:P], ACT.Copy).then_inc(s_nmc, 1)

                def body(i, last_body):
                    for q in range(U // 2):
                        g = i * (U // 2) + q
                        if not (last_body and q == U // 2 - 1):
                            spread(g + 1, q + 1, i * 2 + (q + 1) // PAIRS + 1)
                        act.wait_ge(s_v4, g * K4 + SHIFTED)
                        nc.scalar.activation(exs[q % 2], sc[q % 2], ACT.Exp, scale=float(D) ** -0.5).then_inc(s_ex, 1)
                        if q % PAIRS == 2 and not (last_body and q // PAIRS == 1):
                            mask(i * 2 + q // PAIRS + 1, (q // PAIRS + 1) % 2)
                act.wait_ge(s_k4, 4 + GS)
                mask(0, 0)
                spread(0, 0, 1)
                body(0, False)
                with act.Fori(1, NBODY - 1) as i:
                    body(i, False)
                body(NBODY - 1, True)

            @block.vector
            def _(dve):
                sz = Steps(dve, s_k4v)
                sz.do(nc.vector.memset(acc, 0.0))
                sz.do(nc.vector.memset(ohpad[0], 0.0))
                sz.do(nc.vector.memset(nm[0], 0.0))
                sz.do(nc.vector.memset(nm[1], 0.0))
                sz.do(nc.vector.memset(tiny[:], 0.0))
                sz.link(nc.vector.memset(ohpad[1], 0.0))

                def onehots(grp, b):
                    r = rec_in[b][:].bitcast(F32).rearrange("p (t w) -> p t w", w=4)
                    dve.wait_ge(s_rec[b], (grp - b) * 8 + 16)
                    local = r[:, :, 1:2].to_broadcast([P, GS, WIN])
                    nc.vector.tensor_tensor(ohpad[b][:, :, 0:WIN], local, iota[:, 0:WIN].unsqueeze(1).to_broadcast([P, GS, WIN]), ALU.is_equal)
                    nc.vector.tensor_tensor(nm[b][:, 0:GS * WIN].rearrange("p (t s) -> p t s", t=GS), local,
                                            iota[:, 0:WIN].unsqueeze(1).to_broadcast([P, GS, WIN]), ALU.not_equal)
                    nc.vector.tensor_tensor(typ[b], r[:, :, 2:3].to_broadcast([P, GS, TYPES]),
                                            iota[:, 0:TYPES].unsqueeze(1).to_broadcast([P, GS, TYPES]), ALU.is_equal).then_inc(s_oh4, 1)
                    dve.wait_ge(s_oh4, grp + 1)

                def add_sums(st, g, q):
                    dve.wait_ge(s_pv, g + 1)
                    for t in range(2):
                        w = dve.value_load(mapsb[0:1, bass.ds(g * 2 + t, 1)], min_val=0, max_val=NW - 1)
                        to = acc[:, bass.ds(w * AW, AW)]
                        st.link(nc.vector.tensor_tensor(to, to, PS[5 + q % 2][0:C8, t * 64:t * 64 + AW], ALU.add))

                def body(i, last_body):
                    for q in range(U // 2):
                        g = i * (U // 2) + q
                        b = q % 2
                        st = Steps(dve, s_v4, g * K4)
                        s4 = sc[b].rearrange("p (t g h) -> p t g h", t=2, g=H)
                        e4 = exs[b].rearrange("p (t g h) -> p t g h", t=2, g=H)
                        byhead = [P, 2, H, H]
                        dve.wait_ge(s_s, g + 1)
                        st.link(nc.vector.tensor_reduce(sc[b].rearrange("p (a h) -> p a h", h=H),
                                                        SB[b].rearrange("p (a s h) -> p a h s", s=WIN, h=H), AX.X, ALU.max))
                        st.link(nc.vector.tensor_reduce(top[:].rearrange("p (t h) -> p t h", t=2),
                                                        s4.rearrange("p t g h -> p t h g"), AX.X, ALU.max))
                        st.link(nc.vector.tensor_tensor(s4, s4, top[:].rearrange("p (t h) -> p t h", t=2).unsqueeze(2).to_broadcast(byhead), ALU.subtract))
                        assert st.n == SHIFTED
                        if isinstance(g, int) and g == 0:
                            st.link(nc.vector.memset(tiny[:], 0.0))
                            st.link(nc.vector.memset(tiny[:], 0.0))
                        else:
                            add_sums(st, g - 1, q + 1)
                        if q % PAIRS == 1 and not (last_body and q // PAIRS == 1):
                            onehots(i * 2 + q // PAIRS + 1, (q // PAIRS + 1) % 2)
                        dve.wait_ge(s_ex, g + 1)
                        st.link(nc.vector.tensor_reduce(den[:].rearrange("p (t h) -> p t h", t=2), e4.rearrange("p t g h -> p t h g"), AX.X, ALU.add))
                        st.link(nc.vector.reciprocal(den[:], den[:]))
                        st.link(nc.vector.tensor_tensor(e4, e4, den[:].rearrange("p (t h) -> p t h", t=2).unsqueeze(2).to_broadcast(byhead), ALU.mult))
                        for t in range(2):
                            oh = ohpad[q // PAIRS][:, (2 * q + t) % GS, 0:WIN]
                            st.do(nc.vector.tensor_tensor(em[b][:, t].rearrange("p g (s h) -> p g s h", s=WIN),
                                                          e4[:, t].unsqueeze(2).to_broadcast([P, H, WIN, H]),
                                                          oh.unsqueeze(1).unsqueeze(3).to_broadcast([P, H, WIN, H]), ALU.mult))
                        st.need(st.n)
                        assert st.n == K4, st.n
                onehots(0, 0)
                body(0, False)
                with dve.Fori(1, NBODY - 1) as i:
                    body(i, False)
                body(NBODY - 1, True)
                add_sums(Steps(dve, s_v4, NPAIR * K4), NPAIR - 1, 1)

            @block.tensor
            def _(pe):
                def transposes(g, q, grp):
                    ge(pe, s_ktc, g)
                    for t in range(2):
                        slot = (2 * q + t) % GS
                        pe.wait_ge(s_kv[slot], grp * 16 + 16)
                        for half in range(2):
                            last = nc.tensor.transpose(PS[4][:, t * 256 + half * P:t * 256 + (half + 1) * P],
                                                       kv_in[slot][:, half * P:(half + 1) * P], ident[:])
                    last.then_inc(s_kt, 1)

                def scores(g, q, grp):
                    b = q % 2
                    if q % PAIRS == 0:
                        pe.wait_ge(s_nmc, grp + 1)
                    pe.wait_ge(s_bq, g + 1)
                    pe.wait_ge(s_ktc, g + 1)
                    ge(pe, s_v4, (g - 2) * K4 + REDUCED)
                    for t in range(2):
                        tile = (2 * q + t) % GS
                        o = SB[b][:, t * 512:(t + 1) * 512]
                        nc.tensor.matmul(o, nmT[q // PAIRS % 2], masksel[:, tile * C8:(tile + 1) * C8].unsqueeze(1).to_broadcast([GS * WIN, H, C8]),
                                         start=True, stop=False)
                        for half in range(2):
                            last = nc.tensor.matmul(o[:, half * 256:(half + 1) * 256], kT[b][:, t * 256 + half * P:t * 256 + (half + 1) * P],
                                                    bq_[b][:, t].rearrange("p j c -> p (j c)"), start=False, stop=half == 1)
                    last.then_inc(s_s, 1)

                def values(g, q):
                    b = q % 2
                    pe.wait_ge(s_v4, g * K4 + K4)
                    for t in range(2):
                        slot = (2 * q + t) % GS
                        o = PS[5 + b][0:C8, t * 64:t * 64 + D]
                        for k in range(H):
                            nc.tensor.matmul(o, em[b][:, t, k, :], kv_in[slot][:, HD + D * k:HD + D * (k + 1)], start=k == 0, stop=k == H - 1)
                        last = nc.tensor.matmul(PS[5 + b][0:C8, t * 64 + D:t * 64 + AW], ohpad[q // PAIRS % 2][:, slot, :],
                                                typ[q // PAIRS % 2][:, slot, :], start=True, stop=True)
                    last.then_inc(s_pv, 1)

                def mask(grp, b):
                    pe.wait_ge(s_oh4, grp + 1)
                    ge(pe, s_nmc, grp)
                    nc.tensor.transpose(PSM[:, 0:P], nm[b], identb[:]).then_inc(s_nmt, 1)

                def body(i, last_body):
                    for q in range(U // 2):
                        g = i * (U // 2) + q
                        scores(g, q, i * 2 + q // PAIRS)
                        if not (last_body and q == U // 2 - 1):
                            transposes(g + 1, q + 1, i * 2 + (q + 1) // PAIRS)
                        if not (isinstance(g, int) and g == 0):
                            values(g - 1, (q - 1) % (U // 2))
                        if q % PAIRS == 2 and not (last_body and q // PAIRS == 1):
                            mask(i * 2 + q // PAIRS + 1, (q // PAIRS + 1) % 2)
                pe.wait_ge(s_k4, 4 + GS)
                pe.wait_ge(s_k4v, 6)
                mask(0, 0)
                transposes(0, 0, 0)
                body(0, False)
                with pe.Fori(1, NBODY - 1) as i:
                    body(i, False)
                body(NBODY - 1, True)
                values(NPAIR - 1, U // 2 - 1)

        if stop == 4:
            dump(nc, ctx, dbg, [], [(msg_tab[k * P:(k + 1) * P], k) for k in range(4)] + [(cnt_tab[k * P:(k + 1) * P], 4 + k) for k in range(4)])
            return

        CW = NCH * P
        acc1 = arena[:, 0:NACC * P]

        def finish(kind):
            f = [sortbuf[:, CW * k:CW * (k + 1)] for k in range(11)]
            xin, hin_, wk, sq, res = f[0], f[1], f[2], f[3], f[4]
            msg_in, msgT = sortbuf[:, CW * 5:CW * 7], sortbuf[:, CW * 7:CW * 9]
            mT, hout = f[9], f[10]
            cnt_in, cntT = cnt_in_s, cntT_s
            n3 = [P, NCH, P]

            def v3(a):
                return a.rearrange("p (k f) -> p k f", k=NCH)

            def rows(tab, c, cols=P):
                return tab[bass.ds(c * CW, CW), :].rearrange("(k p) f -> p k f", p=P)

            s_in = sem(f"s_fin{kind}_in")
            s_t = sem(f"s_fin{kind}_transposed")
            s_a = sem(f"s_fin{kind}_act")
            s_m = sem(f"s_fin{kind}_products")
            s_v = sem(f"s_fin{kind}_steps")
            s_o = sem(f"s_fin{kind}_stored")
            dense = kind < 2
            LN = kind != 1
            KY = {0: 2, 1: 4, 2: 3}[kind]
            KV = {0: 2 + 8 + 3, 1: 4 + 3, 2: 3 + 1 + 8}[kind]
            KX = {0: 10, 1: 4, 2: 12}[kind]
            KVAR = {0: 2 + 5, 2: 4 + 5}.get(kind)
            ACTS = {0: 6 + 1 + 2, 1: 2, 2: 2}[kind]
            NIN = {0: 3, 1: 1, 2: 2}[kind]
            NOUT = {0: 2, 1: 1, 2: 1}[kind]
            NTR = {0: 2, 1: 1, 2: 0}[kind]

            def body_sp(sp, c):
                ge(sp, s_v, c * KV)
                if kind == 0:
                    sp.dma_start(msg_in.rearrange("p (k f) -> p k f", k=NCH), rows(msg_tab, c)).then_inc(s_in, 16)
                    sp.dma_start(cnt_in, rows(cnt_tab, c)).then_inc(s_in, 16)
                    sp.dma_start(v3(xin), rows(xpad, c)).then_inc(s_in, 16)
                else:
                    sp.dma_start(v3(hin_), rows(h_tab[kind - 1], c)).then_inc(s_in, 16)
                    if kind == 2:
                        sp.dma_start(v3(xin), rows(x1_tab, c)).then_inc(s_in, 16)
                if kind == 0:
                    sp.wait_ge(s_v, c * KV + KX)
                    sp.dma_start(rows(x1_tab, c), v3(res)).then_inc(s_o, 16)
                sp.wait_ge(s_v, c * KV + KV)
                sp.dma_start(rows(h_tab[kind] if dense else outpad, c), v3(hout if dense else res)).then_inc(s_o, 16)

            def split(bank, a):
                return [(PS[bank][:, 0:512], a[:, 0:512], 0, 4), (PS[bank + 1][:, 0:384], a[:, 512:CW], 4, 7)]

            def body_act(act, c):
                st = Steps(act, s_a, c * ACTS)
                if kind == 0:
                    act.wait_ge(s_t, c * NTR + 1)
                    for k in range(4):
                        w = 512 if k < 3 else 256
                        st.do(nc.scalar.activation(msgT[:, 512 * k:512 * k + w], PS[k][:, 0:w], ACT.Copy))
                    st.do(nc.scalar.activation(cntT[:, 0:512], PS[4][0:TYPES, 0:512], ACT.Copy))
                    st.do(nc.scalar.activation(cntT[:, 512:CW], PS[5][0:TYPES, 0:384], ACT.Copy))
                if kind == 2:
                    act.wait_ge(s_v, c * KV + KY)
                    st.do(nc.scalar.activation(wk, sq, ACT.Sigmoid))
                if LN:
                    act.wait_ge(s_v, c * KV + KVAR)
                    st.do(nc.scalar.activation(stat[:, 16:16 + NCH], stat[:, 8:8 + NCH], ACT.Sqrt, bias=eps_c[:], scale=1.0 / P))
                if dense:
                    act.wait_ge(s_t, c * NTR + NTR)
                    for ps, to, _, _ in split(0, mT):
                        st.do(nc.scalar.activation(to, ps, ACT.Copy))
                assert st.n == ACTS

            def body_pe(pe, c):
                if kind == 0:
                    pe.wait_ge(s_in, c * (16 * NIN) + 16 * NIN)
                    ge(pe, s_a, c * ACTS)
                    for k in range(NCH):
                        for half in range(2):
                            nc.tensor.transpose(PS[k // 2][:, (k % 2) * 256 + half * P:(k % 2) * 256 + (half + 1) * P],
                                                msg_in[:, k * HD + half * P:k * HD + (half + 1) * P], ident[:])
                        last = nc.tensor.transpose(PS[4 + k // 4][0:TYPES, (k % 4) * P:(k % 4 + 1) * P], cnt_in[:, k, :], ident[:])
                    last.then_inc(s_t, 1)
                    pe.wait_ge(s_a, c * ACTS + 6)
                    ge(pe, s_v, c * KV)
                    for k in range(NCH):
                        o = PS[6 + k // 4][:, (k % 4) * P:(k % 4 + 1) * P]
                        for half in range(2):
                            nc.tensor.matmul(o, msgT[:, k * HD + half * P:k * HD + (half + 1) * P], woT[:, half, :], start=half == 0, stop=False)
                        last = nc.tensor.matmul(o, cntT[:, k * P:(k + 1) * P], ebo[:], start=False, stop=True)
                    last.then_inc(s_m, 1)
                if dense:
                    pe.wait_ge(s_v, c * KV + KX)
                    ge(pe, s_a, c * ACTS)
                    for k in range(NCH):
                        last = nc.tensor.transpose(PS[k // 4][:, (k % 4) * P:(k % 4 + 1) * P], res[:, k * P:(k + 1) * P], ident[:])
                    last.then_inc(s_t, 1)
                    pe.wait_ge(s_a, c * ACTS + ACTS)
                    for k in range(NCH):
                        last = nc.tensor.matmul(PS[2 + k // 4][:, (k % 4) * P:(k % 4 + 1) * P], mT[:, k * P:(k + 1) * P], w12T[:, kind, :], start=True, stop=True)
                    last.then_inc(s_m, 1)

            def body_dve(dve, c):
                st = Steps(dve, s_v, c * KV)
                dv = dinv[:, bass.ds(c * NCH, NCH)].unsqueeze(2).to_broadcast(n3)
                dve.wait_ge(s_in, c * (16 * NIN) + 16 * NIN)
                ge(dve, s_o, c * (16 * NOUT))
                if kind == 0:
                    dve.wait_ge(s_m, c * 2 + 1)
                    for ps, to, k0, k1 in split(6, wk):
                        st.link(nc.vector.tensor_tensor(to, ps, xin[:, k0 * P:k1 * P], ALU.add))
                else:
                    st.link(nc.vector.tensor_tensor(sq, acc1[:, bass.ds(c * CW, CW)], hin_, ALU.add))
                    st.link(nc.vector.tensor_tensor(v3(sq), v3(sq), dv, ALU.mult))
                    if kind == 1:
                        st.link(nc.vector.tensor_scalar(res, sq, 0.0, None, ALU.max))
                    st.link(nc.vector.memset(stat[:, 0:1], 0.0))
                    if kind == 2:
                        dve.wait_ge(s_a, c * ACTS + 1)
                        st.link(nc.vector.tensor_tensor(wk, wk, xin, ALU.add))
                assert st.n == KY + (kind == 2)
                if LN:
                    mean = stat[:, 0:NCH]
                    st.link(nc.vector.tensor_reduce(mean, v3(wk), AX.X, ALU.add))
                    st.link(nc.vector.tensor_scalar(mean, mean, 1.0 / P, None, ALU.mult))
                    st.link(nc.vector.tensor_tensor(v3(wk), v3(wk), mean.unsqueeze(2).to_broadcast(n3), ALU.subtract))
                    st.link(nc.vector.tensor_tensor(sq, wk, wk, ALU.mult))
                    st.link(nc.vector.tensor_reduce(stat[:, 8:8 + NCH], v3(sq), AX.X, ALU.add))
                    assert st.n == KVAR
                    dve.wait_ge(s_a, c * ACTS + (7 if kind == 0 else 2))
                    st.link(nc.vector.reciprocal(stat[:, 24:24 + NCH], stat[:, 16:16 + NCH]))
                    st.link(nc.vector.tensor_tensor(v3(res), v3(wk), stat[:, 24:24 + NCH].unsqueeze(2).to_broadcast(n3), ALU.mult))
                    st.link(nc.vector.memset(stat[:, 0:1], 0.0))
                assert st.n == KX, (kind, st.n)
                if dense:
                    dve.wait_ge(s_m, c * (2 if kind == 0 else 1) + (2 if kind == 0 else 1))
                    for ps, to, k0, k1 in split(2, hout):
                        st.link(nc.vector.tensor_tensor(to.rearrange("p (k f) -> p k f", f=P), ps.rearrange("p (k f) -> p k f", f=P),
                                                        b12[:, kind, :].unsqueeze(1).to_broadcast([P, k1 - k0, P]), ALU.add))
                    st.link(nc.vector.tensor_tensor(v3(hout), v3(hout), dv, ALU.mult))
                assert st.n == KV

            with nc.Block() as block:
                @block.sync
                def _(sp):
                    body_sp(sp, 0)
                    with sp.Fori(1, NB // NCH) as c:
                        body_sp(sp, c)
                    sp.wait_ge(s_o, (NB // NCH) * 16 * NOUT)
                    if kind == 2:
                        sp.dma_start(out, outpad[0:N, :]).then_inc(s_out, 16)
                        sp.wait_ge(s_out, 16)

                @block.scalar
                def _(act):
                    body_act(act, 0)
                    with act.Fori(1, NB // NCH) as c:
                        body_act(act, c)

                @block.vector
                def _(dve):
                    body_dve(dve, 0)
                    with dve.Fori(1, NB // NCH) as c:
                        body_dve(dve, c)

                @block.tensor
                def _(pe):
                    if dense:
                        body_pe(pe, 0)
                        with pe.Fori(1, NB // NCH) as c:
                            body_pe(pe, c)

        cntT_s = arena[0:TYPES, 0:CW]
        cnt_in_s = arena[:, CW:CW + NCH * TYPES].rearrange("p (k t) -> p k t", k=NCH)
        stat = sb("stat", [P, 32])
        s_out = sem("s_out")
        finish(0)
        if stop == 5:
            dump(nc, ctx, dbg, [], [(x1_tab[k * P:(k + 1) * P], k) for k in range(4)] + [(h_tab[0][k * P:(k + 1) * P], 4 + k) for k in range(4)])
            return

        at1 = NACC * P
        minb, rel, dkey, m0, m1 = (arena[:, at1 + k * TC * P:at1 + (k + 1) * TC * P] for k in range(5))
        at1 += 5 * TC * P
        rows_in = [arena[:, at1 + P * k:at1 + P * (k + 1)] for k in range(8)]
        at1 += 8 * P
        ohw = [arena[:, at1 + P * k:at1 + P * (k + 1)] for k in range(4)]
        at1 += 4 * P
        assert at1 <= NW * AW
        boff = sortbuf[0:1, 0:TC * P].bitcast(I32)
        idx = [sortbuf[:, TC * P + GE * k:TC * P + GE * (k + 1)].bitcast(I32) for k in range(2)]
        U1 = 2 * GE

        def aggregate(layer):
            s_min = sem(f"s_gcn{layer}_least_in")
            s_pre = sem(f"s_gcn{layer}_prepared")
            s_ix = sem(f"s_gcn{layer}_indices")
            s_g = [sem(f"s_gcn{layer}_rows{k}") for k in range(8)]
            s_mm = sem(f"s_gcn{layer}_products")
            s_oh = sem(f"s_gcn{layer}_onehots")
            s_ad = sem(f"s_gcn{layer}_added")
            s_ps = sem(f"s_gcn{layer}_pass_steps")
            s_go1 = sem(f"s_gcn{layer}_pool_goes_on")
            s_go1d = sem(f"s_gcn{layer}_dve_goes_on")
            NPASS = 5

            with nc.Block() as block:
                @block.sync
                def _(sp):
                    sp.dma_start(minb, bcast_rows(min_row, P, TC * P)).then_inc(s_min, 16)
                    sp.wait_ge(s_min, 16)

                @block.gpsimd
                def _(pool):
                    with pool.Fori(0, pool.value_load(passes[0:1, 0:1], min_val=1, max_val=NB)) as r:
                        with pool.Fori(0, T // U1) as i:
                            for t in range(U1):
                                n = r * T + i * U1 + t
                                u = t // GE
                                if t % GE == 0:
                                    grp = r * (T // GE) + i * 2 + u
                                    pool.wait_ge(s_mm, n + 1)
                                    nc.gpsimd.tensor_copy(idx[u], srcI[:, bass.ds(i * U1 + t, GE)]).then_inc(s_ix, 1)
                                    pool.wait_ge(s_ix, grp + 1)
                                pool.wait_ge(s_mm, n + 1)
                                pool.sem_inc(s_go1, 1)
                                nc.gpsimd.indirect_dma_start(rows_in[t % 8], None, h_tab[layer],
                                                             bass.IndirectOffsetOnAxis(ap=idx[u][:, t % GE:t % GE + 1], axis=0)).then_inc(s_g[t % 8], 16)

                @block.vector
                def _(dve):
                    st = Steps(dve, s_pre)
                    st.do(nc.vector.memset(acc1, 0.0))
                    dve.wait_ge(s_min, 16)
                    if layer == 0:
                        st.link(nc.vector.tensor_scalar(dloT[:], dloT[:], 1.0, None, ALU.add))
                    st.link(nc.vector.tensor_copy(boff, minb[0:1, :]))
                    st.link(nc.vector.tensor_scalar(boff, boff, 7, 7, ALU.arith_shift_right, ALU.logical_shift_left))
                    mi = m1.bitcast(I32)
                    st.link(nc.vector.tensor_copy(mi, minb))
                    st.link(nc.vector.tensor_scalar(mi, mi, P - 1, None, ALU.bitwise_and))
                    st.link(nc.vector.tensor_copy(m0, mi))
                    st.link(nc.vector.tensor_scalar(m0, m0, pcol[:], None, ALU.is_le))
                    st.link(nc.vector.tensor_scalar(m1, m0, -1.0, 1.0, ALU.mult, ALU.add))
                    st.link(nc.vector.tensor_tensor(rel, dstT[:], minb, ALU.subtract))
                    dve.sem_inc(s_ad, 4)
                    with dve.Fori(0, dve.value_load(passes[0:1, 0:1], min_val=1, max_val=NB)) as r:
                        sp_ = Steps(dve, s_ps, r * NPASS)
                        sp_.link(nc.vector.scalar_tensor_tensor(dkey, rel, float(P), dloT[:], ALU.is_lt, ALU.mult))
                        sp_.link(nc.vector.scalar_tensor_tensor(dkey, rel, 0.0, dkey, ALU.is_ge, ALU.mult))
                        sp_.link(nc.vector.tensor_scalar(dkey, dkey, -1.0, None, ALU.add))
                        sp_.link(nc.vector.tensor_scalar(rel, rel, -float(P), None, ALU.add))
                        sp_.do(nc.vector.memset(tiny[:], 0.0))
                        with dve.Fori(0, T // U1) as i:
                            def onehot(t):
                                n = r * T + i * U1 + t
                                col = bass.ds(i * U1 + t, 1)
                                dve.wait_ge(s_mm, n + 5)
                                nc.vector.tensor_scalar(ohw[t % 4], iota[:], dkey[:, col], wT[:, col], ALU.is_equal, ALU.mult).then_inc(s_oh, 1)

                            def add(t):
                                n = r * T + i * U1 + t
                                col = bass.ds(i * U1 + t, 1)
                                v = dve.value_load(boff[0:1, col], min_val=0, max_val=(NB - 1) * P)
                                dve.wait_ge(s_mm, n + 9)
                                dve.wait_ge(s_ad, n + 4)
                                for k, m in enumerate((m0, m1)):
                                    to = acc1[:, bass.ds(v + r * P + k * P, P)]
                                    last = nc.vector.scalar_tensor_tensor(to, PS[t % 4][:, 0:P], m[:, col], to, ALU.mult, ALU.add)
                                last.then_inc(s_ad, 1)
                            for t in range(U1 + 2):
                                if t < U1:
                                    onehot(t)
                                if t >= 2:
                                    add(t - 2)
                        dve.wait_ge(s_ad, r * T + T + 4)
                        dve.sem_inc(s_go1d, 1)

                @block.tensor
                def _(pe):
                    pe.sem_inc(s_mm, 8)
                    with pe.Fori(0, pe.value_load(passes[0:1, 0:1], min_val=1, max_val=NB)) as r:
                        with pe.Fori(0, T // U1) as i:
                            for t in range(U1):
                                n = r * T + i * U1 + t
                                pe.wait_ge(s_g[t % 8], (r * (T // 8) + i * 2 + t // 8) * 16 + 16)
                                pe.wait_ge(s_oh, n + 1)
                                pe.wait_ge(s_ad, n + 1)
                                nc.tensor.matmul(PS[t % 4][:, 0:P], ohw[t % 4], rows_in[t % 8], start=True, stop=True).then_inc(s_mm, 1)

        for layer in range(2):
            aggregate(layer)
            if stop == 6:
                dump(nc, ctx, dbg, [acc1[:, 0:2048]])
                return
            finish(layer + 1)

def bcast_rows(v, rows, cols, at=0):
    return v[at:at + cols].unsqueeze(0).to_broadcast([rows, cols])


def dump(nc, ctx, dbg, aps, drams=()):
    s = ctx.enter_context(nc.semaphore("s_dbg"))
    with nc.Block() as block:
        @block.sync
        def _(sp):
            n = 0
            for i, a in enumerate(aps):
                sp.dma_start(dbg[i, 0:a.shape[0], 0:a.shape[1]], a).then_inc(s, 16)
                n += 16
            for a, i in drams:
                sp.dma_start(dbg[i, 0:a.shape[0], 0:a.shape[1]], a).then_inc(s, 16)
                n += 16
            sp.wait_ge(s, n)


def kernel(**inputs):
    import numpy as np
    import concourse.bacc as bacc
    from concourse.bass_utils import run_bass_kernel_spmd

    names = ["x", "src", "dst", "edge_type_3", "edge_weight1"]
    names += ["L0_gnn_" + k for k in ("Wq", "bq", "Wk", "bk", "Wv", "bv", "edge_emb", "Wo", "bo")]
    names += ["L1_gnn_" + k for k in ("W1", "b1", "W2", "b2")]
    nc = bacc.Bacc("TRN2", target_bir_lowering=False, num_devices=1)
    arrays, args = {}, []
    for name in names:
        a = np.ascontiguousarray(inputs[name])
        if name == "edge_weight1":
            a = a.reshape(-1)
        arrays["in_" + name] = a
        args.append(nc.dram_tensor("in_" + name, a.shape, mybir.dt.from_np(a.dtype), kind="ExternalInput").ap())
    out = nc.dram_tensor("out", (N, P), F32, kind="ExternalOutput").ap()
    gnn_kernel(nc, *args, out)
    return run_bass_kernel_spmd(nc, [arrays], core_ids=[0]).results[0]["out"]
```

```python
import concourse.bass as bass
from concourse import mybir
from contextlib import ExitStack

F32, I32, BF16 = mybir.dt.float32, mybir.dt.int32, mybir.dt.bfloat16
ALU = mybir.AluOpType
ACT = mybir.ActivationFunctionType
AX = mybir.AxisListType

P = 128
N = 6250
E = 206250
NB = 49
NP = NB * P
WIN = 8
NW = NP // WIN
HI, LO = 25, 32
GT = 16
T = -(-E // (P * GT)) * GT
NG = T // GT
TC = -(-T // P)
H, D, HD = 8, 32, 256
TYPES = 3
GS = 8
NTILE = -(-(E // P + NW + (T * P - E) // P + 1) // GS) * GS
MC = -(-NTILE // P)
AW = D + TYPES
GE = 8
BIG = 1.0e30
EPS = 1e-5
PAD_SRC, PAD_DST = N + 14, NP - 1
NCH = 7
NACC = 2 * NB + 1


class Steps:

    def __init__(self, eng, sem, base=0):
        self.eng, self.sem, self.base, self.n = eng, sem, base, 0

    def do(self, ins):
        self.n += 1
        ins.then_inc(self.sem, 1)
        return self.n

    def need(self, n):
        self.eng.wait_ge(self.sem, self.base + n)

    def link(self, ins):
        self.need(self.do(ins))


def gnn_kernel(nc, x, src, dst, etype, ew, Wq, bq, Wk, bk, Wv, bv, emb, Wo, bo, W1, b1, W2, b2, out):
    ctx = ExitStack()
    with ctx:
        def sb(name, shape, dt=F32):
            return ctx.enter_context(nc.sbuf_tensor(name, shape, dt))

        def sem(name):
            return ctx.enter_context(nc.semaphore(name))

        def dram(name, shape, dt=F32):
            return nc.dram_tensor(name, shape, dt).ap()

        def load_row(eng, row, at, n, top):
            return nc.values_load_multi_w_load_instructions(row[0:1, bass.ds(at, n)], engines=(eng.engine,), min_val=0, max_val=top)[1]

        def ge(eng, s, v):
            if not isinstance(v, int) or v > 0:
                eng.wait_ge(s, v)

        xpad2 = dram("xpad", (NP + P, P))
        xpad = xpad2[0:NP, :]
        kv_tab = dram("kv_tab", (NP, 2 * HD))
        qt_tab = dram("qt_tab", (NW, P, WIN * H))
        win_row = dram("win_row", (TC * P * P,))
        hi_row = dram("hi_row", (TC * P * P,))
        recs = dram("recs", (NTILE * P, 4), I32)
        start_row = dram("start_row", (HI * LO,))
        map_row = dram("map_row", (P * MC,), I32)
        msg_tab = dram("msg_tab", (NP, HD))
        cnt_tab = dram("cnt_tab", (NP, TYPES))
        x1_tab = dram("x1_tab", (NP, P))
        h_tab = [dram("h1_tab", (NP, P)), dram("h2_tab", (NP, P))]
        min_row = dram("min_row", (TC * P,))
        max_row = dram("max_row", (TC * P,))
        keep_row = dram("keep_row", (P, 4 * TC * P))
        outpad = dram("outpad", (NP, P))

        ident = sb("ident", [P, P])
        identb = sb("identb", [P, P], BF16)
        iota_i = sb("iota_i", [P, P], I32)
        iota = sb("iota", [P, P])
        pcol = sb("pcol", [P, 1])
        pcol_i = sb("pcol_i", [P, 1], I32)
        npcol = sb("npcol", [P, 1])
        tri = sb("tri", [P, P])
        triT = sb("triT", [P, P])
        eps_c = sb("eps_c", [P, 1])
        zero_b = sb("zero_b", [P, LO], BF16)

        wqkvT = sb("wqkvT", [P, 3, HD])
        woT = sb("woT", [P, 2, P])
        w12T = sb("w12T", [P, 2, P])
        embT = sb("embT", [P, 2, TYPES])
        ebo = sb("ebo", [TYPES, P])
        b12 = sb("b12", [P, 2, P])

        keepbuf = sb("keepbuf", [P, 4 * TC * P])
        dstT, wT, dloT = (keepbuf[:, k * TC * P:(k + 1) * TC * P] for k in range(3))
        srcI = keepbuf[:, 3 * TC * P:].bitcast(I32)
        sortbuf = sb("sortbuf", [P, 6 * TC * P])
        localT, typeT, winT, loT, hiT = (sortbuf[:, k * TC * P:(k + 1) * TC * P] for k in range(5))
        tmpT = sortbuf[:, 5 * TC * P:].bitcast(I32)
        dinv = sb("dinv", [P, NB])
        maprow = sb("maprow", [1, P * MC], I32)
        mapsb = maprow[:, :]

        arena = sb("arena", [P, NW * AW])

        def carve(at, n, dt=F32):
            return arena[:, at:at + n] if dt is F32 else arena[:, at:at + n].bitcast(dt)

        raw = carve(0, 4 * TC * P, I32).rearrange("p (a c e) -> p a c e", a=4, c=TC)
        rawf = carve(4 * TC * P, 4 * TC * P).rearrange("p (a c e) -> p a c e", a=4, c=TC)
        digs = carve(8 * TC * P, 2 * TC * P, I32).rearrange("p (a c) -> p a c", a=2)
        hif = carve(10 * TC * P, TC * P).rearrange("p (c e) -> p c e", c=TC)
        span = sb("span", [P, 2 * TC])
        wraw = sb("wraw", [P, 12, P])
        psum = ctx.enter_context(nc.psum_tensor("psum", [P, 8 * 512], F32))
        PS = [psum[:, 512 * i:512 * (i + 1)] for i in range(8)]
        SB = [psum[:, 0:1024], psum[:, 1024:2048]]
        PSM = PS[7].bitcast(BF16)
        FULL = E // P
        REST = E - FULL * P
        LC = TC - 1
        LROWS = FULL - LC * P

        s_c = sem("s_const")
        s_ld = sem("s_loaded")
        s_wl = sem("s_weights_loaded")
        s_rawf = sem("s_rawf")
        s_tp = sem("s_transposed")
        s_tc = sem("s_transposed_copied")
        s_d1 = sem("s_dve1")
        s_pad = sem("s_pad")
        s_dr = sem("s_rows_stored")
        s_embT = sem("s_embT")
        s_ebo = sem("s_ebo_ready")
        s_zp = sem("s_zero_pad")
        s_mm = sem("s_least_targets")

        with nc.Block() as block:
            @block.gpsimd
            def _(pool):
                st = Steps(pool, s_c)
                st.do(nc.gpsimd.memset(ident[:], 0.0))
                st.do(nc.gpsimd.memset(tri[:], 1.0))
                st.do(nc.gpsimd.memset(triT[:], 1.0))
                st.do(nc.gpsimd.memset(eps_c[:], EPS))
                st.do(nc.gpsimd.memset(zero_b[:], 0.0))
                st.do(nc.gpsimd.iota(iota_i[:], pattern=[[1, P]], base=0, channel_multiplier=0))
                st.link(nc.gpsimd.iota(pcol_i[:], pattern=[[0, 1]], base=0, channel_multiplier=1))
                st.do(nc.gpsimd.affine_select(out=ident[:], in_=ident[:], compare_op=ALU.not_equal, fill=1.0,
                                              base=0, pattern=[[-1, P]], channel_multiplier=1))
                st.do(nc.gpsimd.affine_select(out=tri[:], in_=tri[:], compare_op=ALU.is_gt, fill=0.0,
                                              base=0, pattern=[[-1, P]], channel_multiplier=1))
                st.do(nc.gpsimd.affine_select(out=triT[:], in_=triT[:], compare_op=ALU.is_gt, fill=0.0,
                                              base=0, pattern=[[1, P]], channel_multiplier=-1))
                st.do(nc.gpsimd.tensor_copy(iota[:], iota_i[:]))
                st.link(nc.gpsimd.tensor_copy(pcol[:], pcol_i[:]))
                st.do(nc.gpsimd.tensor_scalar(npcol[:], pcol[:], -1.0, None, ALU.mult))
                st.do(nc.gpsimd.tensor_copy(identb[:], ident[:]))

            NCONST = 14

            @block.sync
            def _(sp):
                for a, (v, dt) in enumerate(((src, I32), (dst, I32), (etype, I32), (ew, F32))):
                    to = raw[:, a] if dt is I32 else rawf[:, a]
                    sp.dma_start(to[:, 0:LC, :], v[0:LC * P * P].rearrange("(c t e) -> t c e", t=P, e=P)).then_inc(s_ld, 16)
                    if a == 0:
                        sp.wait_ge(s_pad, 4)
                    sp.dma_start(to[0:LROWS, LC, :],
                                 v[LC * P * P:FULL * P].rearrange("(t e) -> t e", e=P)).then_inc(s_ld, 16)
                    sp.dma_start(to[LROWS:LROWS + 1, LC, 0:REST],
                                 v[FULL * P:E].rearrange("(t e) -> t e", t=1)).then_inc(s_ld, 16)
                sp.wait_ge(s_rawf, 2)
                sp.dma_start(win_row.rearrange("(c t e) -> t c e", t=P, e=P), rawf[:, 0]).then_inc(s_dr, 16)
                sp.wait_ge(s_rawf, 4)
                sp.dma_start(hi_row.rearrange("(c t e) -> t c e", t=P, e=P), hif).then_inc(s_dr, 16)
                sp.wait_ge(s_mm, 2)
                sp.dma_start(min_row.rearrange("(c t) -> t c", t=P), span[:, 0:TC], allow_slow_non_contiguous=True).then_inc(s_dr, 16)
                sp.dma_start(max_row.rearrange("(c t) -> t c", t=P), span[:, TC:2 * TC], allow_slow_non_contiguous=True).then_inc(s_dr, 16)
                sp.wait_ge(s_dr, 64)

            @block.scalar
            def _(act):
                for i, w in enumerate((Wq, Wk, Wv)):
                    act.dma_start(wraw[:, 2 * i:2 * i + 2, :], w.rearrange("(a p) f -> p a f", p=P)).then_inc(s_wl, 16)
                act.dma_start(wraw[:, 6:8, :], Wo.rearrange("o (a f) -> o a f", f=P)).then_inc(s_wl, 16)
                act.dma_start(wraw[:, 8, :], W1).then_inc(s_wl, 16)
                act.dma_start(wraw[:, 9, :], W2).then_inc(s_wl, 16)
                act.dma_start(wraw[0:TYPES, 10:12, :], emb.rearrange("t (a f) -> t a f", f=P)).then_inc(s_wl, 16)
                act.dma_start(b12[:, 0, :], bcast_rows(b1, P, P)).then_inc(s_wl, 16)
                act.dma_start(b12[:, 1, :], bcast_rows(b2, P, P)).then_inc(s_wl, 16)
                act.dma_start(ebo[:], bcast_rows(bo, TYPES, P)).then_inc(s_wl, 16)
                act.dma_start(xpad2[0:N, :], x).then_inc(s_wl, 16)
                act.wait_ge(s_zp, 1)
                act.dma_start(xpad2[N:NP, :], tmpT[0:NP - N, 0:P].bitcast(F32)).then_inc(s_wl, 16)
                act.dma_start(xpad2[NP:, :], tmpT[:, 0:P].bitcast(F32)).then_inc(s_wl, 16)
                act.wait_ge(s_wl, 13 * 16)

            @block.vector
            def _(dve):
                st = Steps(dve, s_d1)
                nc.vector.memset(raw[:, 0, LC, :], PAD_SRC).then_inc(s_pad, 1)
                nc.vector.memset(raw[:, 1, LC, :], PAD_DST).then_inc(s_pad, 1)
                nc.vector.memset(raw[:, 2, LC, :], 0).then_inc(s_pad, 1)
                nc.vector.memset(rawf[:, 3, LC, :], 0.0).then_inc(s_pad, 1)
                nc.vector.memset(tmpT, 0).then_inc(s_zp, 1)
                dve.wait_ge(s_ld, 12 * 16)
                st.link(nc.vector.tensor_scalar(digs[:, 0, :], raw[:, 0].rearrange("p c e -> p (c e)"), 3, None,
                                                ALU.arith_shift_right))
                nc.vector.tensor_copy(rawf[:, 0].rearrange("p c e -> p (c e)"), digs[:, 0, :]).then_inc(s_rawf, 1)
                dve.wait_ge(s_rawf, 1)
                st.link(nc.vector.tensor_copy(rawf[:, 1], raw[:, 1]))
                nc.vector.tensor_copy(rawf[:, 2], raw[:, 2]).then_inc(s_rawf, 1)
                dve.wait_ge(s_rawf, 2)
                st.link(nc.vector.tensor_scalar(digs[:, 1, :], raw[:, 0].rearrange("p c e -> p (c e)"), 7, None,
                                                ALU.bitwise_and))
                nc.vector.tensor_copy(raw[:, 0].bitcast(F32).rearrange("p c e -> p (c e)"), digs[:, 1, :]).then_inc(s_rawf, 1)
                st.link(nc.vector.tensor_scalar(digs[:, 0, :], digs[:, 0, :], 5, None, ALU.arith_shift_right))
                nc.vector.tensor_copy(hif.rearrange("p c e -> p (c e)"), digs[:, 0, :]).then_inc(s_rawf, 1)
                n = 0
                for target in (winT, dstT, typeT, wT, localT):
                    for c in range(0, TC, 4):
                        k = min(4, TC - c)
                        dve.wait_ge(s_tp, n + 1)
                        nc.vector.tensor_copy(target[:, c * P:(c + k) * P], PS[n % 4][:, 0:k * P]).then_inc(s_tc, 1)
                        n += 1
                nT = n
                for g in range(3):
                    dve.wait_ge(s_tp, n + 1)
                    n += 1
                    if g == 0:
                        nc.vector.tensor_copy(wqkvT[:].rearrange("p a f -> p (a f)")[:, 0:512], PS[(n - 1) % 4][:, :]).then_inc(s_tc, 1)
                    elif g == 1:
                        nc.vector.tensor_copy(wqkvT[:, 2, :], PS[(n - 1) % 4][:, 0:256]).then_inc(s_embT, 1)
                        nc.vector.tensor_copy(woT[:].rearrange("p a f -> p (a f)"), PS[(n - 1) % 4][:, 256:512]).then_inc(s_tc, 1)
                    else:
                        nc.vector.tensor_copy(w12T[:].rearrange("p a f -> p (a f)"), PS[(n - 1) % 4][:, 0:256]).then_inc(s_embT, 1)
                        nc.vector.tensor_copy(embT[:], PS[(n - 1) % 4][:, 256:512].rearrange("p (a t) -> p a t", a=2)[:, :, 0:TYPES]).then_inc(s_tc, 1)
                dve.wait_ge(s_wl, 13 * 16)
                dve.wait_ge(s_ebo, 1)
                st.link(nc.vector.tensor_tensor(ebo[:], PS[4][0:TYPES, 0:P], ebo[:], ALU.add))
                dve.wait_ge(s_tc, nT + 3)
                st.link(nc.vector.tensor_copy(tmpT[:], winT[:]))
                st.link(nc.vector.tensor_scalar(digs[:, 0, :], tmpT[:], 5, None, ALU.arith_shift_right))
                st.do(nc.vector.tensor_copy(hiT[:], digs[:, 0, :]))
                st.link(nc.vector.tensor_scalar(digs[:, 1, :], tmpT[:], 31, None, ALU.bitwise_and))
                st.link(nc.vector.tensor_copy(loT[:], digs[:, 1, :]))
                lo_c, hi_c = span[:, 0:TC], span[:, TC:2 * TC]
                nc.vector.tensor_reduce(lo_c, rawf[:, 1], AX.X, ALU.min).then_inc(s_mm, 1)
                nc.vector.tensor_reduce(hi_c, rawf[:, 1], AX.X, ALU.max).then_inc(s_mm, 1)

            @block.tensor
            def _(pe):
                pe.wait_ge(s_c, NCONST)
                n = 0
                for a in (0, 1, 2, 3, "local"):
                    pe.wait_ge(s_rawf, 3 if a == "local" else 2)
                    if a == 3:
                        pe.wait_ge(s_ld, 12 * 16)
                    for c in range(0, TC, 4):
                        if n >= 4:
                            pe.wait_ge(s_tc, n - 3)
                        for k in range(min(4, TC - c)):
                            frm = raw[:, 0].bitcast(F32)[:, c + k, :] if a == "local" else rawf[:, a, c + k, :]
                            last = nc.tensor.transpose(PS[n % 4][:, k * P:(k + 1) * P], frm, ident[:])
                        last.then_inc(s_tp, 1)
                        n += 1
                pe.wait_ge(s_wl, 13 * 16)
                for g in range(3):
                    pe.wait_ge(s_tc, n - 3)
                    for k in range(4):
                        i = 4 * g + k
                        if i < 10:
                            last = nc.tensor.transpose(PS[n % 4][:, k * P:(k + 1) * P], wraw[:, i, :], ident[:])
                        else:
                            last = nc.tensor.transpose(PS[n % 4][:, k * P:k * P + TYPES], wraw[0:TYPES, i, :], ident[0:TYPES, 0:TYPES])
                    last.then_inc(s_tp, 1)
                    n += 1
                pe.wait_ge(s_tc, n)
                pe.wait_ge(s_embT, 2)
                nc.tensor.matmul(PS[4][0:TYPES, 0:P], embT[:, 0, :], woT[:, 0, :], start=True, stop=False)
                nc.tensor.matmul(PS[4][0:TYPES, 0:P], embT[:, 1, :], woT[:, 1, :], start=False, stop=True).then_inc(s_ebo, 1)

        kvb = sb("kvb", [P, 2 * HD])
        bq4 = sb("bq4", [H, 4, D])
        bqT = sb("bqT", [P, H])
        wq4 = carve(0, H * P).rearrange("p (h r d) -> p h r d", h=H, r=4)
        xt_in = carve(1024, P)
        xT = carve(1280, P)
        kv_out = carve(1408, 2 * HD)
        qt_out = carve(1920, P * H)
        ohlo = [carve(3072 + 256 * i, 256, BF16).rearrange("p (t d) -> p t d", t=GT) for i in range(2)]
        ohhi = [carve(3584 + 256 * i, 200, BF16).rearrange("p (t d) -> p t d", t=GT) for i in range(2)]
        prefill = carve(4096, 2400, I32)
        startb = carve(6500, NW)
        junk = carve(7300, NW)
        tau_i = carve(8100, MC, I32)
        tau = carve(8120, MC)
        mapf = carve(8140, MC)
        map_i = carve(8160, MC, I32)
        ntile_i = carve(8200, LO, I32)
        ntile = carve(8240, LO)
        incl = carve(8280, LO)
        ones_r = carve(8320, LO)
        start = carve(8360, LO)
        carry = sb("carry", [HI, LO])
        lomax = carve(8400, 2 * T)[0:1]
        lomaxg = carve(8400 + 2 * T, 2 * (T // GE))[0:1]
        passes = sb("passes", [1, 1], I32)

        s_k2 = sem("s_kvq_consts")
        s_b2 = sem("s_biases_loaded")
        s_bqp = sem("s_bq_transposed")
        s_bqc = sem("s_bq_copied")
        s_xin = sem("s_x_in")
        s_xp = sem("s_x_transposed")
        s_xc = sem("s_xT_copied")
        s_kvp = sem("s_kv_product")
        s_kvc = sem("s_kv_biased")
        s_qp = sem("s_q_product")
        s_qc = sem("s_q_biased")
        s_kvs = sem("s_kv_stored")
        s_qs = sem("s_q_stored")
        s_oh = sem("s_onehots")
        s_cn = sem("s_counted")
        s_hb = sem("s_hi_base")
        s_p2 = sem("s_prefix")
        s_st = sem("s_starts_stored")
        s_stb = sem("s_starts_back")
        s_map = sem("s_map")
        s_maps = sem("s_map_stored")
        s_rp = sem("s_prefill")
        s_rps = sem("s_prefilled")
        s_tau = sem("s_tau")
        s_wm = sem("s_widest_row")

        with nc.Block() as block:
            @block.sync
            def _(sp):
                sp.dma_start(kvb[:, 0:HD], bcast_rows(bk, P, HD)).then_inc(s_b2, 16)
                sp.dma_start(kvb[:, HD:], bcast_rows(bv, P, HD)).then_inc(s_b2, 16)
                for r in range(4):
                    sp.dma_start(bq4[:, r, :], bq.rearrange("(h d) -> h d", h=H)).then_inc(s_b2, 16)
                sp.dma_start(xt_in, xpad[0:P, :]).then_inc(s_xin, 16)
                sp.dma_start(lomax[:, 0:T], min_row[0:T].unsqueeze(0)).then_inc(s_wm, 16)
                sp.dma_start(lomax[:, T:2 * T], max_row[0:T].unsqueeze(0)).then_inc(s_wm, 16)
                sp.wait_ge(s_rp, 4)
                for k in range(4):
                    r = NTILE * P // 4
                    sp.dma_start(recs[k * r:(k + 1) * r, :].rearrange("(p r) w -> p (r w)", p=P), prefill).then_inc(s_rps, 16)

                xnext = xpad2[P:P + NP, :]
                def body(i):
                    sp.wait_ge(s_xp, i + 1)
                    sp.dma_start(xt_in, xnext[bass.ds(i * P, P), :]).then_inc(s_xin, 16)
                    sp.wait_ge(s_kvc, i + 1)
                    sp.dma_start(kv_tab[bass.ds(i * P, P), :], kv_out).then_inc(s_kvs, 16)
                    sp.wait_ge(s_qc, i * H + H)
                    sp.dma_start(qt_tab[bass.ds(i * GT, GT), :, :].rearrange("w p c -> p w c"),
                                 qt_out.rearrange("p (w c) -> p w c", w=GT)).then_inc(s_qs, 16)
                body(0)
                with sp.Fori(1, NB) as i:
                    body(i)
                sp.wait_ge(s_xin, 16 * (NB + 1))
                sp.wait_ge(s_kvs, 16 * NB)
                sp.wait_ge(s_qs, 16 * NB)
                sp.wait_ge(s_p2, 6)
                sp.dma_start(start_row.rearrange("(h l) -> h l", h=HI), start[0:HI, :]).then_inc(s_st, 16)
                sp.wait_ge(s_st, 16)
                sp.dma_start(startb, bcast_rows(start_row, P, NW)).then_inc(s_stb, 16)
                sp.wait_ge(s_map, MC + 2)
                sp.dma_start(map_row.rearrange("(p c) -> p c", p=P), map_i).then_inc(s_maps, 16)
                sp.wait_ge(s_maps, 16)
                sp.dma_start(mapsb, map_row.unsqueeze(0)).then_inc(s_maps, 16)
                sp.wait_ge(s_maps, 32)
                sp.wait_ge(s_rps, 64)

            @block.gpsimd
            def _(pool):
                rp = Steps(pool, s_rp)
                v = prefill.rearrange("p (r w) -> p r w", w=4)
                rp.do(nc.gpsimd.memset(v[:, :, 0:1], 0))
                rp.do(nc.gpsimd.memset(v.bitcast(F32)[:, :, 1:3], -1.0))
                rp.do(nc.gpsimd.memset(v[:, :, 3:4], 0))
                rp.do(nc.gpsimd.memset(ones_r, 1.0))
                nc.gpsimd.iota(tau_i, pattern=[[1, MC]], base=0, channel_multiplier=MC).then_inc(s_tau, 1)
                pool.wait_ge(s_tau, 1)
                nc.gpsimd.tensor_copy(tau, tau_i).then_inc(s_tau, 1)

            @block.scalar
            def _(act):
                act.wait_ge(s_bqp, 1)
                nc.scalar.activation(bqT[:], PS[5][:, 0:H], ACT.Copy).then_inc(s_bqc, 1)
                act.wait_ge(s_bqc, 1)
                def body(i):
                    act.wait_ge(s_xp, i + 1)
                    nc.scalar.activation(xT, PS[0][:, 0:P], ACT.Copy).then_inc(s_xc, 1)
                    act.wait_ge(s_qp, i + 1)
                    ge(act, s_qs, i * 16)
                    to = qt_out.rearrange("p (n h) -> p n h", h=H)
                    for h in range(H):
                        nc.scalar.activation(to[:, :, h], PS[2 + h // 4][:, (h % 4) * P:(h % 4 + 1) * P], ACT.Identity,
                                             bias=bqT[:, h:h + 1]).then_inc(s_qc, 1)
                body(0)
                with act.Fori(1, NB) as i:
                    body(i)

            @block.vector
            def _(dve):
                nc.vector.tensor_copy(wq4, wqkvT[:, 0, :].rearrange("p (h d) -> p h d", h=H).unsqueeze(2)
                                      .to_broadcast([P, H, 4, D])).then_inc(s_k2, 1)
                dve.wait_ge(s_b2, 6 * 16)
                def kv_bias(i):
                    dve.wait_ge(s_kvp, i + 1)
                    ge(dve, s_kvs, i * 16)
                    nc.vector.tensor_tensor(kv_out, PS[1][:, :], kvb[:], ALU.add).then_inc(s_kvc, 1)
                kv_bias(0)
                with dve.Fori(1, NB) as i:
                    kv_bias(i)
                def onehots(g, b):
                    at = bass.ds(g * GT, GT)
                    nc.vector.tensor_tensor(ohlo[b], loT[:, at].unsqueeze(2).to_broadcast([P, GT, LO]),
                                            iota[:, 0:LO].unsqueeze(1).to_broadcast([P, GT, LO]), ALU.is_equal).then_inc(s_oh, 1)
                    nc.vector.tensor_tensor(ohhi[b], hiT[:, at].unsqueeze(2).to_broadcast([P, GT, HI]),
                                            iota[:, 0:HI].unsqueeze(1).to_broadcast([P, GT, HI]), ALU.is_equal).then_inc(s_oh, 1)
                onehots(0, 0)

                def two_groups(i):
                    ge(dve, s_cn, i * 2)
                    onehots(i * 2 + 1, 1)
                    dve.wait_ge(s_cn, i * 2 + 1)
                    onehots(i * 2 + 2, 0)
                two_groups(0)
                with dve.Fori(1, NG // 2) as i:
                    two_groups(i)
                st = Steps(dve, s_p2)
                dve.wait_ge(s_cn, NG + 1)
                dve.wait_ge(s_rp, 4)
                st.link(nc.vector.tensor_scalar(ntile_i[0:HI, :], PS[4][0:HI, 0:LO], float(P - 1), None, ALU.add))
                st.link(nc.vector.tensor_scalar(ntile_i[0:HI, :], ntile_i[0:HI, :], 7, None, ALU.arith_shift_right))
                st.link(nc.vector.tensor_copy(ntile[0:HI, :], ntile_i[0:HI, :]))
                st.link(nc.vector.tensor_tensor_scan(incl[0:HI, :], ones_r[0:HI, :], ntile[0:HI, :], 0.0, ALU.mult, ALU.add))
                st.link(nc.vector.tensor_tensor(start[0:HI, :], incl[0:HI, :], ntile[0:HI, :], ALU.subtract))
                dve.wait_ge(s_hb, 1)
                st.link(nc.vector.tensor_scalar(start[0:HI, :], start[0:HI, :], PS[5][0:HI, 64:65], None, ALU.add))
                st.link(nc.vector.tensor_scalar(carry[:], start[0:HI, :], float(P), None, ALU.mult))
                dve.wait_ge(s_wm, 32)
                lo_g, hi_g = lomaxg[:, 0:T // GE], lomaxg[:, T // GE:]
                st.do(nc.vector.tensor_reduce(lo_g, lomax[:, 0:T].rearrange("p (g k) -> p g k", k=GE), AX.X, ALU.min))
                st.link(nc.vector.tensor_reduce(hi_g, lomax[:, T:].rearrange("p (g k) -> p g k", k=GE), AX.X, ALU.max))
                st.link(nc.vector.tensor_tensor(hi_g, hi_g, lo_g, ALU.subtract))
                st.link(nc.vector.tensor_reduce(lo_g[:, 0:1], hi_g, AX.X, ALU.max))
                st.link(nc.vector.tensor_scalar(passes[:], lo_g[:, 0:1], float(P), None, ALU.add))
                st.link(nc.vector.tensor_scalar(passes[:], passes[:], 7, None, ALU.arith_shift_right))
                dve.wait_ge(s_stb, 16)
                dve.wait_ge(s_tau, 2)
                mp = Steps(dve, s_map)
                for c in range(MC):
                    mp.link(nc.vector.tensor_scalar(junk, startb, tau[:, c:c + 1], 0.0, ALU.is_le, ALU.add,
                                                    accum_out=mapf[:, c:c + 1]))
                mp.link(nc.vector.tensor_scalar(mapf, mapf, -1.0, None, ALU.add))
                mp.link(nc.vector.tensor_copy(map_i, mapf))

            @block.tensor
            def _(pe):
                pe.wait_ge(s_b2, 6 * 16)
                nc.tensor.transpose(PS[5][:, 0:H], bq4[:].rearrange("h r d -> h (r d)"), ident[0:H, 0:H]).then_inc(s_bqp, 1)
                pe.wait_ge(s_k2, 1)

                def body(i):
                    pe.wait_ge(s_xin, i * 16 + 16)
                    ge(pe, s_xc, i)
                    nc.tensor.transpose(PS[0][:, 0:P], xt_in, ident[:]).then_inc(s_xp, 1)
                    pe.wait_ge(s_xc, i + 1)
                    ge(pe, s_kvc, i)
                    nc.tensor.matmul(PS[1][:, :], xT, wqkvT[:, 1:3, :].rearrange("p a f -> p (a f)"), start=True, stop=True).then_inc(s_kvp, 1)
                    ge(pe, s_qc, i * H)
                    for h in range(H):
                        last = nc.tensor.matmul(PS[2 + h // 4][:, (h % 4) * P:(h % 4 + 1) * P],
                                                wq4[:, h].rearrange("p r d -> p (r d)"), xT, start=True, stop=True)
                    last.then_inc(s_qp, 1)
                body(0)
                with pe.Fori(1, NB) as i:
                    body(i)
                nc.tensor.matmul(PS[4][0:HI, 0:LO], zero_b[:, 0:HI], zero_b[:, 0:LO], start=True, stop=False)

                def count(g, b):
                    pe.wait_ge(s_oh, g * 2 + 2)
                    for t in range(GT):
                        last = nc.tensor.matmul(PS[4][0:HI, 0:LO], ohhi[b][:, t, :], ohlo[b][:, t, :], start=False, stop=False)
                    last.then_inc(s_cn, 1)
                with pe.Fori(0, NG // 2) as i:
                    count(i * 2, 0)
                    count(i * 2 + 1, 1)
                count(NG - 1, 0)
                nc.tensor.matmul(PS[4][0:HI, 0:LO], zero_b[:, 0:HI], zero_b[:, 0:LO], start=False, stop=True).then_inc(s_cn, 1)
                pe.wait_ge(s_p2, 4)
                nc.tensor.matmul(PS[5][0:HI, 64:65], triT[0:HI, 0:HI], incl[0:HI, LO - 1:LO], start=True, stop=True).then_inc(s_hb, 1)

        G2 = GT * P
        win_b = [carve(G2 * i, G2) for i in range(2)]
        hi_b = [carve(G2 * (2 + i), G2) for i in range(2)]
        hiT1 = [carve(G2 * (4 + i), G2) for i in range(2)]
        habs = carve(G2 * 6, G2)
        at = G2 * 7
        dlo_oh = [carve(at + 1024 * i, 1024, BF16).rearrange("p (t d) -> p t d", t=GT) for i in range(2)]
        dhi_oh = [carve(at + 2048 + 392 * i, 392, BF16).rearrange("p (t d) -> p t d", t=GT) for i in range(2)]
        at += 2048 + 784
        ohlo3 = [carve(at + 256 * i, 256, BF16).rearrange("p (t d) -> p t d", t=GT) for i in range(2)]
        ohhi3 = [carve(at + 512 + 200 * i, 200, BF16).rearrange("p (t d) -> p t d", t=GT) for i in range(2)]
        at += 912
        LG = GT + 1
        hin = carve(at, LO * LG).rearrange("p (l t) -> p l t", l=LO)
        keep = carve(at + LO * LG, LO * LG)
        base = [carve(at + (2 + i) * LO * LG, LO * LG).rearrange("p (l t) -> p l t", l=LO) for i in range(2)]
        at += 4 * LO * LG
        looked = carve(at, GT * LO).rearrange("p (t l) -> p t l", t=GT)
        at += GT * LO
        rank = [carve(at + GT * i, GT) for i in range(2)]
        place = carve(at + 2 * GT, GT)
        place_i, pa, pb_ = (carve(at + (3 + i) * GT, GT, I32) for i in range(3))
        addr = [carve(at + (6 + i) * GT, GT, I32) for i in range(2)]
        at += 8 * GT
        rec = [carve(at + 4 * GT * i, 4 * GT, I32).rearrange("p (t w) -> p t w", t=GT) for i in range(2)]
        at += 8 * GT
        same = carve(at, P)
        dhiT = carve(at + P, TC * P)
        dig_i = carve(at + P + TC * P, TC * P, I32)
        dhiT2 = carve(G2 * 7, TC * P)

        s_wb = [sem(f"s_windows_row{i}") for i in range(2)]
        s_hb3 = [sem(f"s_hi_row{i}") for i in range(2)]
        s_ini = sem("s_sort_start")
        s_oh3 = sem("s_onehots3")
        s_hc = sem("s_tile_counts")
        s_h1 = sem("s_hi_onehotT")
        s_v3 = sem("s_sort_steps")
        s_lk = sem("s_bases_looked_up")
        s_dg = sem("s_degree_onehots")
        s_dgc = sem("s_degrees_counted")
        s_sc = [sem(f"s_scattered{i}") for i in range(2)]
        s_sq = sem("s_degree_roots")
        s_go = sem("s_pool_goes_on")
        KR, KS, KM, KA = GT, GT + 3, GT + 5, GT + 15

        with nc.Block() as block:
            @block.sync
            def _(sp):
                def group(g, u, b):
                    sp.wait_ge(s_v3, (g - 2) * KA + KR) if not isinstance(g, int) or g >= 2 else None
                    sp.dma_start(win_b[b], win_row[bass.ds(g * G2, G2)].unsqueeze(0).to_broadcast([P, G2])).then_inc(s_wb[b], 16)
                    sp.wait_ge(s_h1, (g - 2) * 2 + 1) if not isinstance(g, int) or g >= 2 else None
                    sp.dma_start(hi_b[b][0:HI], hi_row[bass.ds(g * G2, G2)].unsqueeze(0).to_broadcast([HI, G2])).then_inc(s_hb3[b], 16)
                group(0, 0, 0)
                group(1, 0, 1)
                with sp.Fori(1, NG // 2) as i:
                    group(i * 2, i, 0)
                    group(i * 2 + 1, i, 1)
                group(NG - 1, 0, 0)

            @block.gpsimd
            def _(pool):
                def group(g, b):
                    pool.wait_ge(s_v3, (g + 1) * KA)
                    pool.sem_inc(s_go, 1)
                    for t in range(GT):
                        nc.gpsimd.indirect_dma_start(recs, bass.IndirectOffsetOnAxis(ap=addr[b][:, t:t + 1], axis=0),
                                                     rec[b][:, t, :], None).then_inc(s_sc[b], 16)
                with pool.Fori(0, NG // 2) as i:
                    group(i * 2, 0)
                    group(i * 2 + 1, 1)
                group(NG - 1, 0)
                pool.wait_ge(s_sc[0], 16 * GT * (NG // 2 + 1))
                pool.wait_ge(s_sc[1], 16 * GT * (NG // 2))

            @block.scalar
            def _(act):
                def group(g, i, b):
                    act.wait_ge(s_hb3[b], i * 16 + 16)
                    ge(act, s_h1, g * 2)
                    nc.scalar.activation(habs[0:HI], hi_b[b][0:HI], ACT.Abs, bias=npcol[0:HI, :]).then_inc(s_h1, 1)
                    act.wait_ge(s_h1, g * 2 + 1)
                    if not isinstance(g, int) or g >= 2:
                        act.wait_ge(s_lk, g - 1)
                    nc.scalar.activation(hiT1[b][0:HI], habs[0:HI], ACT.Relu, bias=1.0, scale=-1.0).then_inc(s_h1, 1)
                group(0, 0, 0)
                group(1, 0, 1)
                with act.Fori(1, NG // 2) as i:
                    group(i * 2, i, 0)
                    group(i * 2 + 1, i, 1)
                group(NG - 1, NG // 2, 0)
                act.wait_ge(s_dgc, NG + 1)
                nc.scalar.activation(dinv[:], PS[2][:, 0:NB], ACT.Sqrt, bias=1.0).then_inc(s_sq, 1)

            @block.vector
            def _(dve):
                si = Steps(dve, s_ini)
                si.do(nc.vector.memset(rec[0], 0))
                si.do(nc.vector.memset(rec[1], 0))
                si.link(nc.vector.tensor_copy(tmpT[:], dstT))
                si.link(nc.vector.tensor_scalar(dig_i, tmpT[:], 7, None, ALU.arith_shift_right))
                si.link(nc.vector.tensor_copy(dhiT, dig_i))
                si.link(nc.vector.tensor_scalar(dig_i, tmpT[:], P - 1, None, ALU.bitwise_and))
                si.link(nc.vector.tensor_copy(dloT, dig_i))
                si.link(nc.vector.tensor_scalar(dig_i, winT, float(WIN), None, ALU.mult))
                si.link(nc.vector.tensor_copy(dhiT2, dig_i))
                si.link(nc.vector.tensor_tensor(srcI, dhiT2, localT, ALU.add))
                si.do(nc.vector.memset(hin[0:HI], 0.0))
                si.link(nc.vector.memset(keep[0:HI], 1.0))
                si.link(nc.vector.memset(keep[0:HI].rearrange("p (l t) -> p l t", l=LO)[:, :, 0:1], 0.0))
                si.link(nc.vector.tensor_copy(base[1][0:HI, :, GT], carry[:]))

                def group(g, i, b):
                    st = Steps(dve, s_v3, g * KA)
                    col = bass.ds(g * GT, GT)
                    later = not isinstance(g, int) or g >= 2
                    if later:
                        dve.wait_ge(s_hc, g - 1)
                    nc.vector.tensor_tensor(ohlo3[b], loT[:, col].unsqueeze(2).to_broadcast([P, GT, LO]),
                                            iota[:, 0:LO].unsqueeze(1).to_broadcast([P, GT, LO]), ALU.is_equal).then_inc(s_oh3, 1)
                    nc.vector.tensor_tensor(ohhi3[b], hiT[:, col].unsqueeze(2).to_broadcast([P, GT, HI]),
                                            iota[:, 0:HI].unsqueeze(1).to_broadcast([P, GT, HI]), ALU.is_equal).then_inc(s_oh3, 1)
                    dve.wait_ge(s_wb[b], i * 16 + 16)
                    for t in range(GT):
                        if t:
                            st.need(t)
                        elif later or g == 1:
                            dve.wait_ge(s_v3, g * KA)
                        st.do(nc.vector.scalar_tensor_tensor(same, win_b[b][:, t * P:(t + 1) * P], winT[:, bass.ds(g * GT + t, 1)],
                                                             tri[:], ALU.is_equal, ALU.mult, accum_out=rank[b][:, t:t + 1]))
                    dve.wait_ge(s_hc, g + 1)
                    st.do(nc.vector.tensor_copy(hin[0:HI, :, 1:LG], PS[b][0:HI, :].rearrange("p (t l) -> p l t", l=LO)))
                    st.link(nc.vector.tensor_copy(hin[0:HI, :, 0], base[1 - b][0:HI, :, GT]))
                    if later:
                        dve.wait_ge(s_lk, g - 1)
                    assert st.n == KR + 2
                    st.do(nc.vector.tensor_tensor_scan(base[b][0:HI].rearrange("p l t -> p (l t)"), keep[0:HI],
                                                       hin[0:HI].rearrange("p l t -> p (l t)"), 0.0, ALU.mult, ALU.add))
                    assert st.n == KS
                    if later:
                        dve.wait_ge(s_dgc, g - 1)
                    nc.vector.tensor_tensor(dlo_oh[b], dloT[:, col].unsqueeze(2).to_broadcast([P, GT, P]),
                                            iota[:].unsqueeze(1).to_broadcast([P, GT, P]), ALU.is_equal).then_inc(s_dg, 1)
                    nc.vector.tensor_tensor(dhi_oh[b], dhiT[:, col].unsqueeze(2).to_broadcast([P, GT, NB]),
                                            iota[:, 0:NB].unsqueeze(1).to_broadcast([P, GT, NB]), ALU.is_equal).then_inc(s_dg, 1)
                    dve.wait_ge(s_lk, g + 1)
                    st.link(nc.vector.tensor_tensor(looked, PS[3 + b][:, :].rearrange("p (t l) -> p t l", t=GT), ohlo3[b], ALU.mult))
                    st.link(nc.vector.tensor_reduce(place, looked, AX.X, ALU.add))
                    assert st.n == KM
                    st.link(nc.vector.tensor_tensor(place, place, rank[b], ALU.add))
                    st.link(nc.vector.tensor_copy(place_i, place))
                    if later:
                        dve.wait_ge(s_sc[b], i * (16 * GT))
                    st.do(nc.vector.tensor_scalar(pa, place_i, 10, 10, ALU.arith_shift_right, ALU.logical_shift_left))
                    st.link(nc.vector.tensor_scalar(pb_, place_i, P - 1, 3, ALU.bitwise_and, ALU.logical_shift_left))
                    st.do(nc.vector.tensor_scalar(place_i, place_i, 7, GS - 1, ALU.arith_shift_right, ALU.bitwise_and))
                    st.link(nc.vector.tensor_tensor(pa, pa, pb_, ALU.bitwise_or))
                    st.do(nc.vector.tensor_copy(rec[b][:, :, 0], dstT[:, col]))
                    st.do(nc.vector.tensor_copy(rec[b][:, :, 1].bitcast(F32), localT[:, col]))
                    st.do(nc.vector.tensor_copy(rec[b][:, :, 2].bitcast(F32), typeT[:, col]))
                    st.link(nc.vector.tensor_tensor(addr[b], pa, place_i, ALU.bitwise_or))
                    assert st.n == KA, st.n
                group(0, 0, 0)
                group(1, 0, 1)
                with dve.Fori(1, NG // 2) as i:
                    group(i * 2, i, 0)
                    group(i * 2 + 1, i, 1)
                group(NG - 1, NG // 2, 0)
                dve.wait_ge(s_sq, 1)
                si.link(nc.vector.reciprocal(dinv[:], dinv[:]))

            @block.tensor
            def _(pe):
                pe.wait_ge(s_ini, 14)

                def group(g, b):
                    pe.wait_ge(s_oh3, g * 2 + 2)
                    if not isinstance(g, int) or g >= 2:
                        pe.wait_ge(s_v3, (g - 2) * KA + KR + 1)
                    for t in range(GT):
                        last = nc.tensor.matmul(PS[b][0:HI, t * LO:(t + 1) * LO], ohhi3[b][:, t, :], ohlo3[b][:, t, :], start=True, stop=True)
                    last.then_inc(s_hc, 1)
                    pe.wait_ge(s_h1, g * 2 + 2)
                    pe.wait_ge(s_v3, g * KA + KS)
                    for t in range(GT):
                        last = nc.tensor.matmul(PS[3 + b][:, t * LO:(t + 1) * LO], hiT1[b][0:HI, t * P:(t + 1) * P], base[b][0:HI, :, t], start=True, stop=True)
                    last.then_inc(s_lk, 1)
                    pe.wait_ge(s_dg, g * 2 + 2)
                    for t in range(GT):
                        last = nc.tensor.matmul(PS[2][:, 0:NB], dlo_oh[b][:, t, :], dhi_oh[b][:, t, :],
                                                start=isinstance(g, int) and g == 0 and t == 0, stop=False)
                    last.then_inc(s_dgc, 1)
                group(0, 0)
                group(1, 1)
                with pe.Fori(1, NG // 2) as i:
                    group(i * 2, 0)
                    group(i * 2 + 1, 1)
                group(NG - 1, 0)
                nc.tensor.matmul(PS[2][:, 0:LO], identb[:], zero_b[:], start=False, stop=True).then_inc(s_dgc, 1)

        U = 2 * GS
        NBODY = NTILE // U
        NPAIR = NTILE // 2
        PAIRS = GS // 2
        C8 = WIN * H

        def spare(at, n, dt=F32):
            v = sortbuf[:, at:at + n]
            return v if dt is F32 else v.bitcast(dt)

        kv_in = [spare(512 * i, 512) for i in range(GS)] + [keepbuf[:, 512 * i:512 * (i + 1)] for i in range(GS)]
        stage = [sb(f"stage{i}", [WIN * H, P]) for i in range(4)]
        kT = [spare(4096 + 512 * i, 512) for i in range(2)]
        qt_in = [spare(5120 + 2 * C8 * i, 2 * C8).rearrange("p (t c) -> p t c", t=2) for i in range(PAIRS)]
        bq_ = [spare(5632 + 512 * i, 512).rearrange("p (t j c) -> p t j c", t=2, j=4) for i in range(2)]
        em = [spare(6656 + 1024 * i, 1024).rearrange("p (t g c) -> p t g c", t=2, g=H) for i in range(2)]
        ohpad = [spare(8704 + 512 * i, 512).rearrange("p (t c) -> p t c", t=GS) for i in range(2)]
        masksel = sb("masksel", [GS * WIN, GS * C8], BF16)
        gmask = sb("gmask", [P, 4])
        rec_in = [sb(f"rec_in{i}", [P, 4 * GS], I32) for i in range(2)]
        small = wraw[:].rearrange("p a f -> p (a f)")
        typ = [small[:, 24 * i:24 * i + 24].rearrange("p (t y) -> p t y", y=TYPES) for i in range(2)]
        nm = [small[:, 64 + 64 * i:128 + 64 * i].bitcast(BF16) for i in range(2)]
        nmT = [small[0:GS * WIN, 192 + 64 * i:256 + 64 * i].bitcast(BF16) for i in range(2)]
        sc = [small[:, 320 + 128 * i:448 + 128 * i] for i in range(2)]
        exs = [small[:, 576 + 128 * i:704 + 128 * i] for i in range(2)]
        top = sb("top", [P, 2 * H])
        den = sb("den", [P, 2 * H])
        tiny = sb("tiny", [1, 2])
        acc = arena[0:C8, :]

        s_k4 = sem("s_l0_consts")
        s_k4v = sem("s_l0_zeroed")
        s_rec = [sem(f"s_records_in{i}") for i in range(2)]
        s_qt = [sem(f"s_queries_in{i}") for i in range(PAIRS)]
        s_kv = [sem(f"s_gathered{i}") for i in range(U)]
        s_bq = sem("s_q_spread")
        s_ktc = sem("s_kT_copied")
        s_kt = sem("s_k_transposed")
        s_s = sem("s_scores")
        s_pv = sem("s_values_summed")
        s_oh4 = sem("s_group_onehots")
        s_nmt = sem("s_mask_transposed")
        s_nmc = sem("s_mask_copied")
        s_v4 = sem("s_softmax_steps")
        s_ex = sem("s_exps")
        s_ms = sem("s_messages_stored")
        s_go4 = sem("s_pool_goes_on4")
        s_sp = sem("s_kept_stored")
        s_st4 = sem("s_sums_staged")
        s_add = sem("s_sums_added")
        LAG = U // 2 + 2
        K4 = 8

        def shifted(g):
            return g * K4 + 3

        def spread_done(g):
            return g * K4 + 9

        def reduced(g):
            return 1 if isinstance(g, int) and g == 0 else g * K4 - 4

        with nc.Block() as block:
            @block.sync
            def _(sp):
                def body(i):
                    for q in range(U // 2):
                        g = i * (U // 2) + q
                        if q % PAIRS == 0:
                            grp = i * 2 + q // PAIRS
                            if not isinstance(i, int):
                                for t in range(GS):
                                    sp.wait_ge(s_kv[q // PAIRS * GS + t], i * 16)
                                sp.wait_ge(s_oh4, grp - 1)
                            sp.dma_start(rec_in[q // PAIRS][:], recs[bass.ds(grp * (P * GS), P * GS), :]
                                         .rearrange("(p t) w -> p (t w)", p=P)).then_inc(s_rec[q // PAIRS], 16)
                        ws = load_row(sp, mapsb, g * 2, 2, NW - 1)
                        ge(sp, s_bq, g - PAIRS + 1)
                        for t, w in enumerate(ws):
                            sp.dma_start(qt_in[q % PAIRS][:, t, :], qt_tab[bass.ds(w, 1), :, :].rearrange("w p c -> (w p) c")).then_inc(s_qt[q % PAIRS], 16)
                sp.dma_start(keep_row, keepbuf[:]).then_inc(s_sp, 16)
                body(0)
                with sp.Fori(1, NBODY) as i:
                    body(i)
                sp.wait_ge(s_pv, NPAIR)
                sp.dma_start(keepbuf[:], keep_row).then_inc(s_sp, 16)
                sp.wait_ge(s_add, NTILE)
                a3 = acc.rearrange("c (w a) -> c w a", a=AW)
                m3 = msg_tab.rearrange("(w s) (h d) -> (s h) w d", s=WIN, h=H)
                for k in range(4):
                    ws = slice(k * (NW // 4), (k + 1) * (NW // 4))
                    sp.dma_start(m3[:, ws, :], a3[:, ws, 0:D]).then_inc(s_ms, 16)
                sp.dma_start(cnt_tab.rearrange("(w s) t -> s w t", s=WIN), a3[0:WIN, :, D:AW]).then_inc(s_ms, 16)
                sp.wait_ge(s_ms, 80)
                sp.wait_ge(s_sp, 32)

            @block.gpsimd
            def _(pool):
                ks = Steps(pool, s_k4)
                ks.link(nc.gpsimd.memset(masksel[:], -BIG))
                for t in range(GS):
                    vt = masksel[:, t * C8:(t + 1) * C8].rearrange("p (s h) -> p s h", s=WIN)
                    ks.do(nc.gpsimd.affine_select(out=vt, in_=vt, compare_op=ALU.is_equal, fill=0.0, base=-WIN * t,
                                                  pattern=[[-1, WIN], [0, H]], channel_multiplier=1))
                ks.link(nc.gpsimd.memset(gmask[:], 1.0))
                ks.link(nc.gpsimd.affine_select(out=gmask[:], in_=gmask[:], compare_op=ALU.is_ge, fill=0.0, base=0,
                                                pattern=[[-D, 4]], channel_multiplier=1))
                ks.link(nc.gpsimd.affine_select(out=gmask[:], in_=gmask[:], compare_op=ALU.is_ge, fill=0.0, base=D - 1,
                                                pattern=[[D, 4]], channel_multiplier=-1))

                def body(i, first, ws):
                    for q in range(U // 2):
                        g = i * (U // 2) + q
                        b = q // PAIRS
                        if q % PAIRS == 0:
                            pool.wait_ge(s_rec[b], i * 16 + 16)
                            pool.sem_inc(s_go4, 1)
                            if isinstance(i, int) and i == 0 and b == 1:
                                pool.wait_ge(s_sp, 16)
                        if not (isinstance(i, int) and i == 0):
                            pool.wait_ge(s_pv, g - U // 2 + 1)
                            pool.sem_inc(s_go4, 1)
                        for t in (2 * q, 2 * q + 1):
                            nc.gpsimd.indirect_dma_start(kv_in[t], None, kv_tab,
                                                         bass.IndirectOffsetOnAxis(ap=rec_in[b][:, 4 * (t % GS):4 * (t % GS) + 1], axis=0)).then_inc(s_kv[t], 16)
                        if q >= first:
                            add_sums(g - LAG, (q - LAG) % 4, ws[2 * (q - first):2 * (q - first) + 2])

                def add_sums(g, b, ws):
                    st = Steps(pool, s_add, g * 2)
                    pool.wait_ge(s_st4, g + 1)
                    pool.sem_inc(s_go4, 1)
                    for t, w in enumerate(ws):
                        to = acc[:, bass.ds(w * AW, AW)]
                        st.link(nc.gpsimd.tensor_tensor(to, to, stage[b][:, t * 64:t * 64 + AW], ALU.add))
                        pool.sem_inc(s_go4, 1)
                body(0, U, None)
                pool.wait_ge(s_k4v, 6)
                body(1, LAG - U // 2, load_row(pool, mapsb, 0, 2 * (U - LAG), NW - 1))
                with pool.Fori(2, NBODY) as i:
                    body(i, 0, load_row(pool, mapsb, i * U - 2 * LAG, U, NW - 1))
                ws = load_row(pool, mapsb, NTILE - 2 * LAG, 2 * LAG, NW - 1)
                for k in range(LAG):
                    add_sums(NPAIR - LAG + k, (k - LAG) % 4, ws[2 * k:2 * k + 2])

            @block.scalar
            def _(act):
                def spread(g, q, uses):
                    ge(act, s_s, g - 1)
                    act.wait_ge(s_qt[q % PAIRS], uses * 32)
                    for j in range(4):
                        last = nc.scalar.activation(bq_[q % 2][:, :, j, :], qt_in[q % PAIRS], ACT.Copy, scale=gmask[:, j:j + 1])
                    last.then_inc(s_bq, 1)
                    act.wait_ge(s_kt, g + 1)
                    nc.scalar.activation(kT[q % 2], PS[4][:, :], ACT.Copy).then_inc(s_ktc, 1)

                def mask(grp, b):
                    act.wait_ge(s_nmt, grp + 1)
                    ge(act, s_s, grp * PAIRS - PAIRS)
                    nc.scalar.activation(nmT[b], PSM[0:GS * WIN, 0:P], ACT.Copy).then_inc(s_nmc, 1)

                def stage_sums(g, b):
                    act.wait_ge(s_pv, g + 1)
                    ge(act, s_add, (g - 3) * 2)
                    nc.scalar.activation(stage[b % 4][:].rearrange("c (t a) -> c t a", t=2)[:, :, 0:AW],
                                         PS[5 + b % 2][0:C8, 0:P].rearrange("c (t a) -> c t a", t=2)[:, :, 0:AW], ACT.Copy).then_inc(s_st4, 1)

                def body(i, last_body):
                    for q in range(U // 2):
                        g = i * (U // 2) + q
                        act.wait_ge(s_v4, shifted(g))
                        nc.scalar.activation(exs[q % 2], sc[q % 2], ACT.Exp, scale=float(D) ** -0.5).then_inc(s_ex, 1)
                        if not (last_body and q >= U // 2 - 2):
                            spread(g + 2, q + 2, i * 2 + (q + 2) // PAIRS + 1)
                        if not (isinstance(g, int) and g < 2):
                            stage_sums(g - 2, q + 2)
                        if q % PAIRS == 2 and not (last_body and q // PAIRS == 1):
                            mask(i * 2 + q // PAIRS + 1, (q // PAIRS + 1) % 2)
                act.wait_ge(s_k4, 4 + GS)
                mask(0, 0)
                spread(0, 0, 1)
                spread(1, 1, 1)
                body(0, False)
                with act.Fori(1, NBODY - 1) as i:
                    body(i, False)
                body(NBODY - 1, True)
                stage_sums(NPAIR - 2, U // 2 - 2)
                stage_sums(NPAIR - 1, U // 2 - 1)

            @block.vector
            def _(dve):
                sz = Steps(dve, s_k4v)
                sz.do(nc.vector.memset(acc, 0.0))
                sz.do(nc.vector.memset(ohpad[0], 0.0))
                sz.do(nc.vector.memset(nm[0], 0.0))
                sz.do(nc.vector.memset(nm[1], 0.0))
                sz.do(nc.vector.memset(tiny[:], 0.0))
                sz.link(nc.vector.memset(ohpad[1], 0.0))

                def onehots(grp, b):
                    r = rec_in[b][:].bitcast(F32).rearrange("p (t w) -> p t w", w=4)
                    dve.wait_ge(s_rec[b], (grp - b) * 8 + 16)
                    local = r[:, :, 1:2].to_broadcast([P, GS, WIN])
                    nc.vector.tensor_tensor(ohpad[b][:, :, 0:WIN], local, iota[:, 0:WIN].unsqueeze(1).to_broadcast([P, GS, WIN]), ALU.is_equal)
                    nc.vector.tensor_tensor(nm[b][:, 0:GS * WIN].rearrange("p (t s) -> p t s", t=GS), local,
                                            iota[:, 0:WIN].unsqueeze(1).to_broadcast([P, GS, WIN]), ALU.not_equal)
                    nc.vector.tensor_tensor(typ[b], r[:, :, 2:3].to_broadcast([P, GS, TYPES]),
                                            iota[:, 0:TYPES].unsqueeze(1).to_broadcast([P, GS, TYPES]), ALU.is_equal).then_inc(s_oh4, 1)
                    dve.wait_ge(s_oh4, grp + 1)

                def scores_of(g, q):
                    b = q % 2
                    dve.wait_ge(s_s, g + 1)
                    return nc.vector.tensor_reduce(sc[b].rearrange("p (a h) -> p a h", h=H),
                                                   SB[b].rearrange("p (a s h) -> p a h s", s=WIN, h=H), AX.X, ALU.max)

                def body(i, last_body):
                    for q in range(U // 2):
                        g = i * (U // 2) + q
                        b = q % 2
                        st = Steps(dve, s_v4, g * K4 + 1)
                        s4 = sc[b].rearrange("p (t g h) -> p t g h", t=2, g=H)
                        e4 = exs[b].rearrange("p (t g h) -> p t g h", t=2, g=H)
                        byhead = [P, 2, H, H]
                        st.link(nc.vector.tensor_reduce(top[:].rearrange("p (t h) -> p t h", t=2),
                                                        s4.rearrange("p t g h -> p t h g"), AX.X, ALU.max))
                        st.do(nc.vector.tensor_tensor(s4, s4, top[:].rearrange("p (t h) -> p t h", t=2).unsqueeze(2).to_broadcast(byhead), ALU.subtract))
                        if last_body and q == U // 2 - 1:
                            st.do(nc.vector.memset(tiny[:], 0.0))
                        else:
                            st.do(scores_of(g + 1, q + 1))
                        if q % PAIRS == 1 and not (last_body and q // PAIRS == 1):
                            ge(dve, s_pv, g - 1)
                            onehots(i * 2 + q // PAIRS + 1, (q // PAIRS + 1) % 2)
                        dve.wait_ge(s_ex, g + 1)
                        st.link(nc.vector.tensor_reduce(den[:].rearrange("p (t h) -> p t h", t=2), e4.rearrange("p t g h -> p t h g"), AX.X, ALU.add))
                        st.link(nc.vector.reciprocal(den[:], den[:]))
                        st.link(nc.vector.tensor_tensor(e4, e4, den[:].rearrange("p (t h) -> p t h", t=2).unsqueeze(2).to_broadcast(byhead), ALU.mult))
                        ge(dve, s_pv, g - 1)
                        for t in range(2):
                            oh = ohpad[q // PAIRS][:, (2 * q + t) % GS, 0:WIN]
                            st.do(nc.vector.tensor_tensor(em[b][:, t].rearrange("p g (s h) -> p g s h", s=WIN),
                                                          e4[:, t].unsqueeze(2).to_broadcast([P, H, WIN, H]),
                                                          oh.unsqueeze(1).unsqueeze(3).to_broadcast([P, H, WIN, H]), ALU.mult))
                        assert st.n == K4, st.n
                onehots(0, 0)
                Steps(dve, s_v4).link(scores_of(0, 0))
                body(0, False)
                with dve.Fori(1, NBODY - 1) as i:
                    body(i, False)
                body(NBODY - 1, True)

            @block.tensor
            def _(pe):
                def transposes(g, q, use):
                    ge(pe, s_ktc, g)
                    for t in range(2):
                        slot = (2 * q + t) % U
                        pe.wait_ge(s_kv[slot], use * 16 + 16)
                        for half in range(2):
                            last = nc.tensor.transpose(PS[4][:, t * 256 + half * P:t * 256 + (half + 1) * P],
                                                       kv_in[slot][:, half * P:(half + 1) * P], ident[:])
                    last.then_inc(s_kt, 1)

                def scores(g, q, grp):
                    b = q % 2
                    if q % PAIRS == 0:
                        pe.wait_ge(s_nmc, grp + 1)
                    pe.wait_ge(s_bq, g + 1)
                    pe.wait_ge(s_ktc, g + 1)
                    if not (isinstance(g, int) and g < 2):
                        pe.wait_ge(s_v4, reduced(g - 2))
                    for t in range(2):
                        tile = (2 * q + t) % GS
                        o = SB[b][:, t * 512:(t + 1) * 512]
                        nc.tensor.matmul(o, nmT[q // PAIRS % 2], masksel[:, tile * C8:(tile + 1) * C8].unsqueeze(1).to_broadcast([GS * WIN, H, C8]),
                                         start=True, stop=False)
                        for half in range(2):
                            last = nc.tensor.matmul(o[:, half * 256:(half + 1) * 256], kT[b][:, t * 256 + half * P:t * 256 + (half + 1) * P],
                                                    bq_[b][:, t].rearrange("p j c -> p (j c)"), start=False, stop=half == 1)
                    last.then_inc(s_s, 1)

                def values(g, q):
                    b = q % 2
                    pe.wait_ge(s_v4, spread_done(g))
                    ge(pe, s_st4, g - 1)
                    for t in range(2):
                        slot, tile = (2 * q + t) % U, (2 * q + t) % GS
                        o = PS[5 + b][0:C8, t * 64:t * 64 + D]
                        for k in range(H):
                            nc.tensor.matmul(o, em[b][:, t, k, :], kv_in[slot][:, HD + D * k:HD + D * (k + 1)], start=k == 0, stop=k == H - 1)
                        last = nc.tensor.matmul(PS[5 + b][0:C8, t * 64 + D:t * 64 + AW], ohpad[q // PAIRS % 2][:, tile, :],
                                                typ[q // PAIRS % 2][:, tile, :], start=True, stop=True)
                    last.then_inc(s_pv, 1)

                def mask(grp, b):
                    pe.wait_ge(s_oh4, grp + 1)
                    ge(pe, s_nmc, grp)
                    nc.tensor.transpose(PSM[:, 0:P], nm[b], identb[:]).then_inc(s_nmt, 1)

                def body(i, last_body):
                    for q in range(U // 2):
                        g = i * (U // 2) + q
                        if not (last_body and q == U // 2 - 1):
                            scores(g + 1, q + 1, i * 2 + (q + 1) // PAIRS)
                        if not (last_body and q >= U // 2 - 2):
                            transposes(g + 2, q + 2, i + (q + 2) // (U // 2))
                        if q % PAIRS == 2 and not (last_body and q // PAIRS == 1):
                            mask(i * 2 + q // PAIRS + 1, (q // PAIRS + 1) % 2)
                        if not (isinstance(g, int) and g == 0):
                            values(g - 1, (q - 1) % (U // 2))
                pe.wait_ge(s_k4, 4 + GS)
                pe.wait_ge(s_k4v, 6)
                mask(0, 0)
                transposes(0, 0, 0)
                scores(0, 0, 0)
                transposes(1, 1, 0)
                body(0, False)
                with pe.Fori(1, NBODY - 1) as i:
                    body(i, False)
                body(NBODY - 1, True)
                values(NPAIR - 1, U // 2 - 1)

        CW = NCH * P
        acc1 = arena[:, 0:NACC * P]

        def finish(kind):
            f = [sortbuf[:, CW * k:CW * (k + 1)] for k in range(11)]
            xin, hin_, wk, sq, res = f[0], f[1], f[2], f[3], f[4]
            msg_in, msgT = sortbuf[:, CW * 5:CW * 7], sortbuf[:, CW * 7:CW * 9]
            mT, hout = f[9], f[10]
            cnt_in, cntT = cnt_in_s, cntT_s
            n3 = [P, NCH, P]

            def v3(a):
                return a.rearrange("p (k f) -> p k f", k=NCH)

            def rows(tab, c, cols=P):
                return tab[bass.ds(c * CW, CW), :].rearrange("(k p) f -> p k f", p=P)

            s_in = sem(f"s_fin{kind}_in")
            s_t = sem(f"s_fin{kind}_transposed")
            s_a = sem(f"s_fin{kind}_act")
            s_m = sem(f"s_fin{kind}_products")
            s_v = sem(f"s_fin{kind}_steps")
            s_o = sem(f"s_fin{kind}_stored")
            dense = kind < 2
            LN = kind != 1
            KY = {0: 2, 1: 4, 2: 3}[kind]
            KV = {0: 2 + 8 + 3, 1: 4 + 3, 2: 3 + 1 + 8}[kind]
            KX = {0: 10, 1: 4, 2: 12}[kind]
            KVAR = {0: 2 + 5, 2: 4 + 5}.get(kind)
            ACTS = {0: 6 + 1 + 2, 1: 2, 2: 2}[kind]
            NIN = {0: 3, 1: 1, 2: 2}[kind]
            NOUT = {0: 2, 1: 1, 2: 1}[kind]
            NTR = {0: 2, 1: 1, 2: 0}[kind]

            def body_sp(sp, c):
                ge(sp, s_v, c * KV)
                if kind == 0:
                    sp.dma_start(msg_in.rearrange("p (k f) -> p k f", k=NCH), rows(msg_tab, c)).then_inc(s_in, 16)
                    sp.dma_start(cnt_in, rows(cnt_tab, c)).then_inc(s_in, 16)
                    sp.dma_start(v3(xin), rows(xpad, c)).then_inc(s_in, 16)
                else:
                    sp.dma_start(v3(hin_), rows(h_tab[kind - 1], c)).then_inc(s_in, 16)
                    if kind == 2:
                        sp.dma_start(v3(xin), rows(x1_tab, c)).then_inc(s_in, 16)
                if kind == 0:
                    sp.wait_ge(s_v, c * KV + KX)
                    sp.dma_start(rows(x1_tab, c), v3(res)).then_inc(s_o, 16)
                sp.wait_ge(s_v, c * KV + KV)
                sp.dma_start(rows(h_tab[kind] if dense else outpad, c), v3(hout if dense else res)).then_inc(s_o, 16)

            def split(bank, a):
                return [(PS[bank][:, 0:512], a[:, 0:512], 0, 4), (PS[bank + 1][:, 0:384], a[:, 512:CW], 4, 7)]

            def body_act(act, c):
                st = Steps(act, s_a, c * ACTS)
                if kind == 0:
                    act.wait_ge(s_t, c * NTR + 1)
                    for k in range(4):
                        w = 512 if k < 3 else 256
                        st.do(nc.scalar.activation(msgT[:, 512 * k:512 * k + w], PS[k][:, 0:w], ACT.Copy))
                    st.do(nc.scalar.activation(cntT[:, 0:512], PS[4][0:TYPES, 0:512], ACT.Copy))
                    st.do(nc.scalar.activation(cntT[:, 512:CW], PS[5][0:TYPES, 0:384], ACT.Copy))
                if kind == 2:
                    act.wait_ge(s_v, c * KV + KY)
                    st.do(nc.scalar.activation(wk, sq, ACT.Sigmoid))
                if LN:
                    act.wait_ge(s_v, c * KV + KVAR)
                    st.do(nc.scalar.activation(stat[:, 16:16 + NCH], stat[:, 8:8 + NCH], ACT.Sqrt, bias=eps_c[:], scale=1.0 / P))
                if dense:
                    act.wait_ge(s_t, c * NTR + NTR)
                    for ps, to, _, _ in split(0, mT):
                        st.do(nc.scalar.activation(to, ps, ACT.Copy))
                assert st.n == ACTS

            def body_pe(pe, c):
                if kind == 0:
                    pe.wait_ge(s_in, c * (16 * NIN) + 16 * NIN)
                    ge(pe, s_a, c * ACTS)
                    for k in range(NCH):
                        for half in range(2):
                            nc.tensor.transpose(PS[k // 2][:, (k % 2) * 256 + half * P:(k % 2) * 256 + (half + 1) * P],
                                                msg_in[:, k * HD + half * P:k * HD + (half + 1) * P], ident[:])
                        last = nc.tensor.transpose(PS[4 + k // 4][0:TYPES, (k % 4) * P:(k % 4 + 1) * P], cnt_in[:, k, :], ident[:])
                    last.then_inc(s_t, 1)
                    pe.wait_ge(s_a, c * ACTS + 6)
                    ge(pe, s_v, c * KV)
                    for k in range(NCH):
                        o = PS[6 + k // 4][:, (k % 4) * P:(k % 4 + 1) * P]
                        for half in range(2):
                            nc.tensor.matmul(o, msgT[:, k * HD + half * P:k * HD + (half + 1) * P], woT[:, half, :], start=half == 0, stop=False)
                        last = nc.tensor.matmul(o, cntT[:, k * P:(k + 1) * P], ebo[:], start=False, stop=True)
                    last.then_inc(s_m, 1)
                if dense:
                    pe.wait_ge(s_v, c * KV + KX)
                    ge(pe, s_a, c * ACTS)
                    for k in range(NCH):
                        last = nc.tensor.transpose(PS[k // 4][:, (k % 4) * P:(k % 4 + 1) * P], res[:, k * P:(k + 1) * P], ident[:])
                    last.then_inc(s_t, 1)
                    pe.wait_ge(s_a, c * ACTS + ACTS)
                    for k in range(NCH):
                        last = nc.tensor.matmul(PS[2 + k // 4][:, (k % 4) * P:(k % 4 + 1) * P], mT[:, k * P:(k + 1) * P], w12T[:, kind, :], start=True, stop=True)
                    last.then_inc(s_m, 1)

            def body_dve(dve, c):
                st = Steps(dve, s_v, c * KV)
                dv = dinv[:, bass.ds(c * NCH, NCH)].unsqueeze(2).to_broadcast(n3)
                dve.wait_ge(s_in, c * (16 * NIN) + 16 * NIN)
                ge(dve, s_o, c * (16 * NOUT))
                if kind == 0:
                    dve.wait_ge(s_m, c * 2 + 1)
                    for ps, to, k0, k1 in split(6, wk):
                        st.link(nc.vector.tensor_tensor(to, ps, xin[:, k0 * P:k1 * P], ALU.add))
                else:
                    st.link(nc.vector.tensor_tensor(sq, acc1[:, bass.ds(c * CW, CW)], hin_, ALU.add))
                    st.link(nc.vector.tensor_tensor(v3(sq), v3(sq), dv, ALU.mult))
                    if kind == 1:
                        st.link(nc.vector.tensor_scalar(res, sq, 0.0, None, ALU.max))
                    st.link(nc.vector.memset(stat[:, 0:1], 0.0))
                    if kind == 2:
                        dve.wait_ge(s_a, c * ACTS + 1)
                        st.link(nc.vector.tensor_tensor(wk, wk, xin, ALU.add))
                assert st.n == KY + (kind == 2)
                if LN:
                    mean = stat[:, 0:NCH]
                    st.link(nc.vector.tensor_reduce(mean, v3(wk), AX.X, ALU.add))
                    st.link(nc.vector.tensor_scalar(mean, mean, 1.0 / P, None, ALU.mult))
                    st.link(nc.vector.tensor_tensor(v3(wk), v3(wk), mean.unsqueeze(2).to_broadcast(n3), ALU.subtract))
                    st.link(nc.vector.tensor_tensor(sq, wk, wk, ALU.mult))
                    st.link(nc.vector.tensor_reduce(stat[:, 8:8 + NCH], v3(sq), AX.X, ALU.add))
                    assert st.n == KVAR
                    dve.wait_ge(s_a, c * ACTS + (7 if kind == 0 else 2))
                    st.link(nc.vector.reciprocal(stat[:, 24:24 + NCH], stat[:, 16:16 + NCH]))
                    st.link(nc.vector.tensor_tensor(v3(res), v3(wk), stat[:, 24:24 + NCH].unsqueeze(2).to_broadcast(n3), ALU.mult))
                    st.link(nc.vector.memset(stat[:, 0:1], 0.0))
                assert st.n == KX, (kind, st.n)
                if dense:
                    dve.wait_ge(s_m, c * (2 if kind == 0 else 1) + (2 if kind == 0 else 1))
                    for ps, to, k0, k1 in split(2, hout):
                        st.link(nc.vector.tensor_tensor(to.rearrange("p (k f) -> p k f", f=P), ps.rearrange("p (k f) -> p k f", f=P),
                                                        b12[:, kind, :].unsqueeze(1).to_broadcast([P, k1 - k0, P]), ALU.add))
                    st.link(nc.vector.tensor_tensor(v3(hout), v3(hout), dv, ALU.mult))
                assert st.n == KV

            with nc.Block() as block:
                @block.sync
                def _(sp):
                    body_sp(sp, 0)
                    with sp.Fori(1, NB // NCH) as c:
                        body_sp(sp, c)
                    sp.wait_ge(s_o, (NB // NCH) * 16 * NOUT)
                    if kind == 2:
                        sp.dma_start(out, outpad[0:N, :]).then_inc(s_out, 16)
                        sp.wait_ge(s_out, 16)

                @block.scalar
                def _(act):
                    body_act(act, 0)
                    with act.Fori(1, NB // NCH) as c:
                        body_act(act, c)

                @block.vector
                def _(dve):
                    body_dve(dve, 0)
                    with dve.Fori(1, NB // NCH) as c:
                        body_dve(dve, c)

                @block.tensor
                def _(pe):
                    if dense:
                        body_pe(pe, 0)
                        with pe.Fori(1, NB // NCH) as c:
                            body_pe(pe, c)

        cntT_s = arena[0:TYPES, 0:CW]
        cnt_in_s = arena[:, CW:CW + NCH * TYPES].rearrange("p (k t) -> p k t", k=NCH)
        stat = sb("stat", [P, 32])
        s_out = sem("s_out")
        finish(0)
        at1 = NACC * P
        minb, rel, dkey = (arena[:, at1 + k * TC * P:at1 + (k + 1) * TC * P] for k in range(3))
        at1 += 3 * TC * P
        ming, m0, m1 = (arena[:, at1 + k * (T // GE):at1 + (k + 1) * (T // GE)] for k in range(3))
        at1 += 3 * (T // GE)
        rows_in = [arena[:, at1 + P * k:at1 + P * (k + 1)] for k in range(8)]
        at1 += 8 * P
        ohw = [arena[:, at1 + P * k:at1 + P * (k + 1)] for k in range(4)]
        at1 += 4 * P
        assert at1 <= NW * AW
        boff = sortbuf[0:1, 0:T // GE].bitcast(I32)
        idx = [sortbuf[:, TC * P + GE * k:TC * P + GE * (k + 1)].bitcast(I32) for k in range(2)]
        U1 = 2 * GE

        def aggregate(layer):
            s_min = sem(f"s_gcn{layer}_least_in")
            s_pre = sem(f"s_gcn{layer}_prepared")
            s_ix = sem(f"s_gcn{layer}_indices")
            s_g = [sem(f"s_gcn{layer}_rows{k}") for k in range(8)]
            s_mm = sem(f"s_gcn{layer}_products")
            s_oh = sem(f"s_gcn{layer}_onehots")
            s_ad = sem(f"s_gcn{layer}_added")
            s_ps = sem(f"s_gcn{layer}_pass_steps")
            s_go1 = sem(f"s_gcn{layer}_pool_goes_on")
            s_go1d = sem(f"s_gcn{layer}_dve_goes_on")
            NPASS = 5

            with nc.Block() as block:
                @block.sync
                def _(sp):
                    sp.dma_start(minb, bcast_rows(min_row, P, TC * P)).then_inc(s_min, 16)
                    sp.wait_ge(s_min, 16)

                @block.gpsimd
                def _(pool):
                    with pool.Fori(0, pool.value_load(passes[0:1, 0:1], min_val=1, max_val=NB)) as r:
                        with pool.Fori(0, T // U1) as i:
                            for t in range(U1):
                                n = r * T + i * U1 + t
                                u = t // GE
                                if t % GE == 0:
                                    grp = r * (T // GE) + i * 2 + u
                                    pool.wait_ge(s_mm, n + 1)
                                    nc.gpsimd.tensor_copy(idx[u], srcI[:, bass.ds(i * U1 + t, GE)]).then_inc(s_ix, 1)
                                    pool.wait_ge(s_ix, grp + 1)
                                pool.wait_ge(s_mm, n + 1)
                                pool.sem_inc(s_go1, 1)
                                nc.gpsimd.indirect_dma_start(rows_in[t % 8], None, h_tab[layer],
                                                             bass.IndirectOffsetOnAxis(ap=idx[u][:, t % GE:t % GE + 1], axis=0)).then_inc(s_g[t % 8], 16)

                @block.vector
                def _(dve):
                    st = Steps(dve, s_pre)
                    st.do(nc.vector.memset(acc1, 0.0))
                    dve.wait_ge(s_min, 16)
                    if layer == 0:
                        st.link(nc.vector.tensor_scalar(dloT, dloT, 1.0, None, ALU.add))
                    st.link(nc.vector.tensor_reduce(ming, minb[:, 0:T].rearrange("p (g k) -> p g k", k=GE), AX.X, ALU.min))
                    st.link(nc.vector.tensor_copy(boff, ming[0:1, :]))
                    st.link(nc.vector.tensor_scalar(boff, boff, 7, 7, ALU.arith_shift_right, ALU.logical_shift_left))
                    mi = m1.bitcast(I32)
                    st.link(nc.vector.tensor_copy(mi, ming))
                    st.link(nc.vector.tensor_scalar(mi, mi, P - 1, None, ALU.bitwise_and))
                    st.link(nc.vector.tensor_copy(m0, mi))
                    st.link(nc.vector.tensor_scalar(m0, m0, pcol[:], None, ALU.is_le))
                    st.link(nc.vector.tensor_scalar(m1, m0, -1.0, 1.0, ALU.mult, ALU.add))
                    st.link(nc.vector.tensor_tensor(rel[:, 0:T].rearrange("p (g k) -> p g k", k=GE), dstT[:, 0:T].rearrange("p (g k) -> p g k", k=GE),
                                                    ming.unsqueeze(2).to_broadcast([P, T // GE, GE]), ALU.subtract))
                    dve.sem_inc(s_ad, 2)
                    with dve.Fori(0, dve.value_load(passes[0:1, 0:1], min_val=1, max_val=NB)) as r:
                        sp_ = Steps(dve, s_ps, r * NPASS)
                        sp_.link(nc.vector.scalar_tensor_tensor(dkey[:, 0:T], rel[:, 0:T], float(P), dloT[:, 0:T], ALU.is_lt, ALU.mult))
                        sp_.link(nc.vector.scalar_tensor_tensor(dkey[:, 0:T], rel[:, 0:T], 0.0, dkey[:, 0:T], ALU.is_ge, ALU.mult))
                        sp_.link(nc.vector.tensor_scalar(dkey[:, 0:T], dkey[:, 0:T], -1.0, None, ALU.add))
                        sp_.link(nc.vector.tensor_scalar(rel[:, 0:T], rel[:, 0:T], -float(P), None, ALU.add))
                        sp_.do(nc.vector.memset(tiny[:], 0.0))
                        with dve.Fori(0, T // U1) as i:
                            offs = load_row(dve, boff, i * 2, 2, (NB - 1) * P)

                            def onehot(t):
                                n = r * T + i * U1 + t
                                col = bass.ds(i * U1 + t, 1)
                                dve.wait_ge(s_mm, n + 5)
                                nc.vector.tensor_scalar(ohw[t % 4], iota[:], dkey[:, col], wT[:, col], ALU.is_equal, ALU.mult).then_inc(s_oh, 1)

                            def add(u):
                                n = r * (T // GE) + i * 2 + u
                                col = bass.ds(i * 2 + u, 1)
                                dve.wait_ge(s_mm, r * T + i * U1 + u * GE + GE + 8)
                                dve.wait_ge(s_ad, n + 2)
                                for k, m in enumerate((m0, m1)):
                                    to = acc1[:, bass.ds(offs[u] + r * P + k * P, P)]
                                    last = nc.vector.scalar_tensor_tensor(to, PS[u][:, 0:P], m[:, col], to, ALU.mult, ALU.add)
                                last.then_inc(s_ad, 1)
                            for t in range(U1):
                                onehot(t)
                                if t == GE + 2:
                                    add(0)
                            add(1)
                        dve.wait_ge(s_ad, r * (T // GE) + T // GE + 2)
                        dve.sem_inc(s_go1d, 1)

                @block.tensor
                def _(pe):
                    pe.sem_inc(s_mm, 8)
                    with pe.Fori(0, pe.value_load(passes[0:1, 0:1], min_val=1, max_val=NB)) as r:
                        with pe.Fori(0, T // U1) as i:
                            for t in range(U1):
                                n = r * T + i * U1 + t
                                pe.wait_ge(s_g[t % 8], (r * (T // 8) + i * 2 + t // 8) * 16 + 16)
                                pe.wait_ge(s_oh, n + 1)
                                if t % GE == 0:
                                    pe.wait_ge(s_ad, r * (T // GE) + i * 2 + t // GE + 1)
                                nc.tensor.matmul(PS[t // GE][:, 0:P], ohw[t % 4], rows_in[t % 8], start=t % GE == 0, stop=t % GE == GE - 1).then_inc(s_mm, 1)

        for layer in range(2):
            aggregate(layer)
            finish(layer + 1)


def bcast_rows(v, rows, cols, at=0):
    return v[at:at + cols].unsqueeze(0).to_broadcast([rows, cols])


def kernel(**inputs):
    import numpy as np
    import concourse.bacc as bacc
    from concourse.bass_utils import run_bass_kernel_spmd

    names = ["x", "src", "dst", "edge_type_3", "edge_weight1"]
    names += ["L0_gnn_" + k for k in ("Wq", "bq", "Wk", "bk", "Wv", "bv", "edge_emb", "Wo", "bo")]
    names += ["L1_gnn_" + k for k in ("W1", "b1", "W2", "b2")]
    nc = bacc.Bacc("TRN2", target_bir_lowering=False, num_devices=1)
    arrays, args = {}, []
    for name in names:
        a = np.ascontiguousarray(inputs[name])
        if name == "edge_weight1":
            a = a.reshape(-1)
        arrays["in_" + name] = a
        args.append(nc.dram_tensor("in_" + name, a.shape, mybir.dt.from_np(a.dtype), kind="ExternalInput").ap())
    out = nc.dram_tensor("out", (N, P), F32, kind="ExternalOutput").ap()
    gnn_kernel(nc, *args, out)
    return run_bass_kernel_spmd(nc, [arrays], core_ids=[0]).results[0]["out"]
```
